# Optimizing a Trainium2 kernel written in Bass

```python
import numpy as np
import jax
import jax.numpy as jnp

def _softmax(x, axis=-1):
    return jax.nn.softmax(x, axis=axis)

def _gelu(x):
    return jax.nn.gelu(x, approximate=True)

def _silu(x):
    return jax.nn.silu(x)

def _sigmoid(x):
    return jax.nn.sigmoid(x)

def _layernorm(x, axis=-1, eps=1e-05):
    m = jnp.mean(x, axis=axis, keepdims=True)
    v = jnp.var(x, axis=axis, keepdims=True)
    return (x - m) / jnp.sqrt(v + eps)

def _scatter_add(tgt, idx, src, axis=0):
    return tgt.at[idx].add(src)

def _segment_sum(src, seg, n):
    return jax.ops.segment_sum(src, seg, n)
kernel_name = 'mk_sandwich_d1_jaxref_r8_4619d5'

def setup_inputs(seed: int=0):
    np.random.seed(seed)
    _w = jnp.asarray

    def _L0_attn_setup():
        import jax, jax.numpy as jnp
        import numpy as np
        B, S, H = (1, 256, 512)
        NH = 32
        QK_NOPE, QK_ROPE, V_DIM = (128, 64, 128)
        Q_LORA, KV_LORA = (192, 64)
        EPS = 1e-06

        def _rms_norm(x, w):
            return x * jax.lax.rsqrt(jnp.mean(x * x, axis=-1, keepdims=True) + EPS) * w

        def _rope_cos_sin(seqlen, dim):
            freqs = 1.0 / 10000.0 ** (jnp.arange(0, dim, 2, dtype=jnp.float32) / dim)
            t = jnp.arange(seqlen, dtype=jnp.float32)
            ang = jnp.outer(t, freqs)
            return (jnp.cos(ang), jnp.sin(ang))

        def _apply_rope(x, cos, sin):
            x1 = x[..., 0::2]
            x2 = x[..., 1::2]
            r1 = x1 * cos - x2 * sin
            r2 = x1 * sin + x2 * cos
            return jnp.stack([r1, r2], axis=-1).reshape(x.shape)
        key = jax.random.key(seed)
        ks = jax.random.split(key, 7)
        s = 0.02
        return {'x': jax.random.normal(ks[0], (B, S, H), jnp.float32), 'wq_a': jax.random.normal(ks[1], (Q_LORA, H), jnp.float32) * s, 'q_norm_w': jnp.ones((Q_LORA,), jnp.float32), 'wq_b': jax.random.normal(ks[2], (NH * (QK_NOPE + QK_ROPE), Q_LORA), jnp.float32) * s, 'wkv_a': jax.random.normal(ks[3], (KV_LORA + QK_ROPE, H), jnp.float32) * s, 'kv_norm_w': jnp.ones((KV_LORA,), jnp.float32), 'wkv_b': jax.random.normal(ks[4], (NH * (QK_NOPE + V_DIM), KV_LORA), jnp.float32) * s, 'wo': jax.random.normal(ks[5], (H, NH * V_DIM), jnp.float32) * s}
    _L0_attn_in = _L0_attn_setup()

    def _L0_ffn_setup():
        import jax, jax.numpy as jnp
        import numpy as np
        DIM = 512
        HIDDEN = 1376
        B, S = (4, 256)

        def _qlinear(x, w_int, scale):
            w = w_int.astype(x.dtype) * scale
            return jnp.einsum('bsd,hd->bsh', x, w)
        key = jax.random.key(seed)
        k_x, k_g, k_u, k_d = jax.random.split(key, 4)
        x = jax.random.normal(k_x, (B, S, DIM), dtype=jnp.float32)
        w_gate = jax.random.randint(k_g, (HIDDEN, DIM), -127, 128, dtype=jnp.int32)
        w_up = jax.random.randint(k_u, (HIDDEN, DIM), -127, 128, dtype=jnp.int32)
        w_down = jax.random.randint(k_d, (DIM, HIDDEN), -127, 128, dtype=jnp.int32)
        scale_gate = jnp.float32(0.01)
        scale_up = jnp.float32(0.01)
        scale_down = jnp.float32(0.01)
        return {'x': x, 'w_gate': w_gate, 'w_up': w_up, 'w_down': w_down, 'scale_gate': scale_gate, 'scale_up': scale_up, 'scale_down': scale_down}
    _L0_ffn_in = _L0_ffn_setup()
    _d = {'L0_attn_x': _L0_attn_in['x'], 'L0_attn_wq_a': _L0_attn_in['wq_a'], 'L0_attn_q_norm_w': _L0_attn_in['q_norm_w'], 'L0_attn_wq_b': _L0_attn_in['wq_b'], 'L0_attn_wkv_a': _L0_attn_in['wkv_a'], 'L0_attn_kv_norm_w': _L0_attn_in['kv_norm_w'], 'L0_attn_wkv_b': _L0_attn_in['wkv_b'], 'L0_attn_wo': _L0_attn_in['wo'], 'L0_ffn_w_gate': _L0_ffn_in['w_gate'], 'L0_ffn_w_up': _L0_ffn_in['w_up'], 'L0_ffn_w_down': _L0_ffn_in['w_down'], 'L0_ffn_scale_gate': _L0_ffn_in['scale_gate'], 'L0_ffn_scale_up': _L0_ffn_in['scale_up'], 'L0_ffn_scale_down': _L0_ffn_in['scale_down']}
    _x0 = _d['L0_attn_x']
    _d['L0_attn_x'] = jax.random.normal(jax.random.fold_in(jax.random.key(seed), 1), (2, 1024, 512), dtype=_x0.dtype)
    del _x0
    return _d

def reference(L0_attn_x, L0_attn_wq_a, L0_attn_q_norm_w, L0_attn_wq_b, L0_attn_wkv_a, L0_attn_kv_norm_w, L0_attn_wkv_b, L0_attn_wo, L0_ffn_w_gate, L0_ffn_w_up, L0_ffn_w_down, L0_ffn_scale_gate, L0_ffn_scale_up, L0_ffn_scale_down):

    def _L0_attn_ref(x, wq_a, q_norm_w, wq_b, wkv_a, kv_norm_w, wkv_b, wo):
        import jax, jax.numpy as jnp
        import numpy as np
        B, S, H = (1, 256, 512)
        NH = 32
        QK_NOPE, QK_ROPE, V_DIM = (128, 64, 128)
        Q_LORA, KV_LORA = (192, 64)
        EPS = 1e-06

        def _rms_norm(x, w):
            return x * jax.lax.rsqrt(jnp.mean(x * x, axis=-1, keepdims=True) + EPS) * w

        def _rope_cos_sin(seqlen, dim):
            freqs = 1.0 / 10000.0 ** (jnp.arange(0, dim, 2, dtype=jnp.float32) / dim)
            t = jnp.arange(seqlen, dtype=jnp.float32)
            ang = jnp.outer(t, freqs)
            return (jnp.cos(ang), jnp.sin(ang))

        def _apply_rope(x, cos, sin):
            x1 = x[..., 0::2]
            x2 = x[..., 1::2]
            r1 = x1 * cos - x2 * sin
            r2 = x1 * sin + x2 * cos
            return jnp.stack([r1, r2], axis=-1).reshape(x.shape)
        b, s, _ = x.shape
        cos, sin = _rope_cos_sin(s, QK_ROPE)
        q = _rms_norm(x @ wq_a.T, q_norm_w) @ wq_b.T
        q = q.reshape(b, s, NH, QK_NOPE + QK_ROPE)
        q_nope, q_pe = (q[..., :QK_NOPE], q[..., QK_NOPE:])
        q_pe = _apply_rope(q_pe, cos[None, :, None, :], sin[None, :, None, :])
        kv = x @ wkv_a.T
        kv_c, k_pe = (kv[..., :KV_LORA], kv[..., KV_LORA:])
        k_pe = _apply_rope(k_pe, cos[None, :, :], sin[None, :, :])
        kv_up = _rms_norm(kv_c, kv_norm_w) @ wkv_b.T
        kv_up = kv_up.reshape(b, s, NH, QK_NOPE + V_DIM)
        k_nope, v = (kv_up[..., :QK_NOPE], kv_up[..., QK_NOPE:])
        scale = 1.0 / jnp.sqrt(jnp.float32(QK_NOPE + QK_ROPE))
        scores = (jnp.einsum('bshd,bthd->bhst', q_nope, k_nope) + jnp.einsum('bshd,btd->bhst', q_pe, k_pe)) * scale
        causal = jnp.tril(jnp.ones((s, s), bool))
        scores = jnp.where(causal[None, None], scores, jnp.finfo(scores.dtype).min)
        probs = jax.nn.softmax(scores, axis=-1)
        out = jnp.einsum('bhst,bthd->bshd', probs, v).reshape(b, s, NH * V_DIM)
        return out @ wo.T

    def _L0_ffn_ref(x, w_gate, w_up, w_down, scale_gate, scale_up, scale_down):
        import jax, jax.numpy as jnp
        import numpy as np
        DIM = 512
        HIDDEN = 1376
        B, S = (4, 256)

        def _qlinear(x, w_int, scale):
            w = w_int.astype(x.dtype) * scale
            return jnp.einsum('bsd,hd->bsh', x, w)
        x_gate = _qlinear(x, w_gate, scale_gate)
        x_up = _qlinear(x, w_up, scale_up)
        x_mid = jax.nn.silu(x_gate) * x_up
        x_out = _qlinear(x_mid, w_down, scale_down)
        return x_out
    x = L0_attn_x
    x = x + _layernorm(_L0_attn_ref(_layernorm(x, axis=-1), L0_attn_wq_a, L0_attn_q_norm_w, L0_attn_wq_b, L0_attn_wkv_a, L0_attn_kv_norm_w, L0_attn_wkv_b, L0_attn_wo), axis=-1)
    x = x + _layernorm(_L0_ffn_ref(_layernorm(x, axis=-1), L0_ffn_w_gate, L0_ffn_w_up, L0_ffn_w_down, L0_ffn_scale_gate, L0_ffn_scale_up, L0_ffn_scale_down), axis=-1)
    return x

_drawn_inputs = setup_inputs


def setup_inputs(seed=0):
    import zlib

    import numpy as np

    out = dict(_drawn_inputs(seed))
    spreads = {'L0_attn_q_norm_w': (1.0, 0.582), 'L0_attn_kv_norm_w': (1.0, 0.2)}
    factors = {}
    for name, (base, spread) in spreads.items():
        noise = np.random.default_rng([zlib.crc32(name.encode()), seed]).standard_normal(out[name].shape)
        drawn = base * np.exp(spread * noise) if base else spread * noise
        out[name] = jnp.asarray(drawn.astype(out[name].dtype))
    for name, factor in factors.items():
        out[name] = (out[name] * factor).astype(out[name].dtype)
    return out
```

```python
import concourse.bass as bass
from concourse import mybir
from contextlib import ExitStack

F32 = mybir.dt.float32
F32R = mybir.dt.float32r
I32 = mybir.dt.int32
ALU = mybir.AluOpType
ACT = mybir.ActivationFunctionType

P = 128
BATCH, SEQ, DM = 2, 1024, 512
TOKENS = BATCH * SEQ
NT = TOKENS // P
JT = SEQ // P
KD = DM // P
NH, NOPE, ROPE, VD = 32, 128, 64, 128
QL, KVL = 192, 64
HALF = ROPE // 2
QB = QL - P
AW = QL + KVL + ROPE
GH = 8
NG = NH // GH
GK = GH * KVL // P
HID = 1376
HT = -(-HID // P)
FG = 2
NFG = -(-HT // FG)
TB = 512
NTB = TOKENS // TB
LN_EPS, RMS_EPS = 1e-5, 1e-6
FAR = 1e38


class Lane:

    def __init__(self, reached, sem=None):
        self.reached, self.sem, self.count, self.steps = reached, sem, 0, []
        self.passed = {}

    def need(self, *names):
        self.steps += [("need", n) for n in names if n is not None]

    def go(self, issue, done=None):
        if done is not None:
            assert done not in self.reached, done
            self.count += 1
            self.reached[done] = (self.sem, self.count)
        self.steps.append(("go", issue, self.sem if done is not None else None, 1))

    def load(self, issue, done, sem):
        assert done not in self.reached, done
        n = sem.count = sem.count + 16
        self.reached[done] = (sem, n)
        self.steps.append(("go", issue, sem, 16))

    def play(self, eng):
        for kind, what, *inc in self.steps:
            if kind == "need":
                sem, value = self.reached[what]
                if self.passed.get(sem.name, 0) < value:
                    self.passed[sem.name] = value
                    eng.wait_ge(sem.handle, value)
            else:
                ins = what(eng)
                if inc[0] is not None:
                    ins.then_inc(inc[0].handle, inc[1])
        self.steps = []


class Sem:
    def __init__(self, ctx, nc, name):
        self.name, self.count = name, 0
        self.handle = ctx.enter_context(nc.semaphore(name))


class Core:

    def __init__(self, ctx, nc):
        self.ctx, self.nc, self.reached, self.sems = ctx, nc, {}, {}
        self.pe, self.act, self.dve, self.pool = (
            Lane(self.reached, Sem(ctx, nc, f"s_{n}")) for n in ("pe", "act", "dve", "pool"))
        self.sync = Lane(self.reached)

    def dma_sem(self, name):
        if name not in self.sems:
            self.sems[name] = Sem(self.ctx, self.nc, f"s_{name}")
        return self.sems[name]

    def play(self):
        with self.nc.Block() as block:
            block.sync(self.sync.play)
            block.tensor(self.pe.play)
            block.vector(self.dve.play)
            block.scalar(self.act.play)
            block.gpsimd(self.pool.play)


def f32(ap):
    return ap.bitcast(F32)


def split_passes(a_high, a_low, b_high, b_low):
    return [(a_high, b_high), (a_high, b_low), (a_low, b_high)]


def mm_chain(eng, out, pairs):
    for n, (stationary, moving) in enumerate(pairs):
        ins = eng.matmul(out, stationary, moving, start=n == 0, stop=n == len(pairs) - 1)
    return ins


def layer_kernel(nc, x, wa, wqn, wqp, wk, wv, wo, qw, kvw, rope_k, rope_q, far, wg, wu, wd,
                 sg, su, sd, out):
    weff_dram = nc.dram_tensor("weff", (NH, P, 4 * P), F32R, kind="Internal").ap()
    m_dram = nc.dram_tensor("m_fold", (NG, P, GK * 2 * DM), F32R, kind="Internal").ap()
    x2_dram = nc.dram_tensor("x_mid", (NT, P, DM), F32, kind="Internal").ap()
    x_t = x.rearrange("(n p) d -> n p d", p=P)
    out_t = out.rearrange("(n p) d -> n p d", p=P)

    with ExitStack() as whole:
        core = Core(whole, nc)

        def sb(ctx, name, shape, dt=F32):
            return ctx.enter_context(nc.sbuf_tensor(name, shape, dt))

        def pb(ctx, name, width=512):
            return ctx.enter_context(nc.psum_tensor(name, [P, width], F32))

        ident = sb(whole, "ident", [P, P])
        acc = sb(whole, "acc", [P, NT, DM])
        core.pool.go(lambda e: e.memset(ident[:, :], 0.0), done="ident zero")
        core.pool.need("ident zero")
        core.pool.go(lambda e: e.affine_select(
            out=ident[:, :], in_=ident[:, :], compare_op=ALU.not_equal, fill=1.0, base=0,
            pattern=[[-1, P]], channel_multiplier=1), done="ident")

        with ExitStack() as attn:
            q_lat = {
                "a_high": sb(attn, "qa_high", [P, TOKENS], F32R),
                "a_low": sb(attn, "qa_low", [P, TOKENS], F32R),
                "b_both": sb(attn, "qb_both", [P, TOKENS], F32R),
            }
            k_high = sb(attn, "k_high", [P, TOKENS], F32R)
            k_low = sb(attn, "k_low", [P, TOKENS], F32R)
            lat1 = sb(attn, "lat1", [P, NT, KVL + 1])
            with ExitStack() as ctx:
                latents(core, ctx, sb, pb, ident, x_t, wa, qw, kvw, rope_k, q_lat, k_high, k_low,
                        lat1)
                fold_weights(core, ctx, sb, pb, wqn, wqp, wk, wv, wo, weff_dram, m_dram)
                core.play()
            with ExitStack() as ctx:
                attention(core, ctx, sb, pb, ident, rope_q, far, q_lat, k_high, k_low, lat1,
                          weff_dram, m_dram, acc)
                core.play()
        with ExitStack() as ctx:
            feed_forward(core, ctx, sb, pb, ident, x_t, x2_dram, acc, wg, wu, wd, sg, su, sd,
                         out_t)
            core.play()


def latents(core, ctx, sb, pb, ident, x_t, wa, qw, kvw, rope_k, q_lat, k_high, k_low, lat1):
    pe, act, dve, pool, sync = core.pe, core.act, core.dve, core.pool, core.sync
    wa_raw = sb(ctx, "wa_raw", [P, KD, AW])
    wa_high = sb(ctx, "wa_high", [P, KD, AW], F32R)
    wa_low = sb(ctx, "wa_low", [P, KD, AW], F32R)
    qw_col = sb(ctx, "qw_col", [P, 2])
    kvw_row = sb(ctx, "kvw_row", [P, KVL])
    rk = sb(ctx, "rope_k_sb", [P, JT, 4 * HALF])
    xin = sb(ctx, "xin", [P, 2, DM])
    stats = sb(ctx, "stats", [P, NT, 6])
    mv = sb(ctx, "mv", [P, NT, 2])
    dev = sb(ctx, "dev", [P, NT])
    rstd = sb(ctx, "rstd", [P, NT])
    xn = sb(ctx, "xn", [P, 2, DM])
    xt_high = sb(ctx, "xt_high", [P, 2, DM], F32R)
    xt_low = sb(ctx, "xt_low", [P, 2, DM], F32R)
    squares = sb(ctx, "squares", [P, QL])
    ssum = sb(ctx, "ssum", [P, NT, 2])
    rms = sb(ctx, "rms", [P, NT, 2])
    rrms = sb(ctx, "rrms", [P, NT, 2])
    qn = sb(ctx, "qn", [P, 2, 2 * P])
    kk = sb(ctx, "kk", [P, 2, P])
    kv2 = sb(ctx, "kv2", [P, 2, ROPE])
    t_ps = [pb(ctx, f"t_ps{i}") for i in range(2)]
    a_ps = [pb(ctx, f"a_ps{i}") for i in range(2)]
    u_ps = [pb(ctx, f"u_ps{i}") for i in range(2)]
    eps = sb(ctx, "eps1", [P, 2])
    dve.go(lambda e: e.memset(eps[:, 0:1], LN_EPS))
    dve.go(lambda e: e.memset(eps[:, 1:2], RMS_EPS), done="eps1")

    sync.load(lambda e: e.dma_start(xin[:, 0, :], x_t[0]), ("x", 0), core.dma_sem("x0"))
    sync.load(lambda e: e.dma_start(wa_raw[:, :, :], wa.rearrange("(k p) n -> p k n", p=P)),
              "wa", core.dma_sem("wa"))
    sync.load(lambda e: e.dma_start(xin[:, 1, :], x_t[1]), ("x", 1), core.dma_sem("x1"))
    for name, dst, src in (("qw", qw_col[:, :], qw),
                           ("kvw", kvw_row[:, :], kvw.to_broadcast((P, KVL))),
                           ("rk", rk[:, :, :], rope_k.rearrange("(j p) n -> p j n", p=P))):
        sync.load(lambda e, dst=dst, src=src: e.dma_start(dst, src), name, core.dma_sem(name))
    dve.go(lambda e: e.memset(lat1[:, :, KVL:KVL + 1], 1.0), done="ones")

    def split_wa():
        act.need("wa")
        act.go(lambda e: e.activation(wa_high[:, :, :], wa_raw[:, :, :], ACT.Copy), done="wa high")
        dve.need("wa high")
        dve.go(lambda e: e.tensor_tensor(wa_low[:, :, :], wa_raw[:, :, :], f32(wa_high[:, :, :]),
                                         ALU.subtract), done="wa low")

    def normalise(i):
        r = i % 2
        if i >= 2:
            sync.need(("xn", i - 2))
            sync.load(lambda e: e.dma_start(xin[:, r, :], x_t[i]), ("x", i), core.dma_sem(f"x{r}"))
        dve.need(("x", i))
        dve.go(lambda e: e.bn_stats(stats[:, i, :], xin[:, r, :]), done=("st", i))
        dve.need(("st", i))
        dve.go(lambda e: e.bn_aggr(mv[:, i, :], stats[:, i, :]), done=("mv", i))
        act.need(("mv", i), "eps1")
        act.go(lambda e: e.activation(dev[:, i:i + 1], mv[:, i, 1:2], ACT.Sqrt,
                                      bias=eps[:, 0:1]), done=("dev", i))
        dve.need(("dev", i))
        dve.go(lambda e: e.reciprocal(rstd[:, i:i + 1], dev[:, i:i + 1]), done=("rstd", i))
        dve.need(("rstd", i))
        if i >= 2:
            dve.need(("T", i - 2))
        dve.go(lambda e: e.tensor_scalar(xn[:, r, :], xin[:, r, :], mv[:, i, 0:1],
                                         rstd[:, i:i + 1], ALU.subtract, ALU.mult),
               done=("xn", i))

    def transpose_x(i):
        r = i % 2
        pe.need(("xn", i), "ident")
        if i >= 2:
            pe.need(("xt low", i - 2))
        def issue(e):
            for k in range(KD):
                ins = e.transpose(t_ps[r][:, k * P:(k + 1) * P], xn[:, r, k * P:(k + 1) * P],
                                  ident[:, :])
            return ins
        pe.go(issue, done=("T", i))
        act.need(("T", i))
        if i >= 2:
            act.need(("A", i - 2))
        act.go(lambda e: e.activation(xt_high[:, r, :], t_ps[r][:, :], ACT.Copy),
               done=("xt high", i))
        dve.need(("xt high", i))
        dve.go(lambda e: e.tensor_tensor(xt_low[:, r, :], t_ps[r][:, :], f32(xt_high[:, r, :]),
                                         ALU.subtract), done=("xt low", i))

    def project(i):
        r = i % 2
        q = a_ps[r]
        pe.need(("xt low", i), "wa low")
        if i >= 2:
            pe.need(("kk2", i - 2))
        pairs = []
        for k in range(KD):
            s = slice(k * P, (k + 1) * P)
            pairs += split_passes(xt_high[:, r, s], xt_low[:, r, s], wa_high[:, k, :],
                                  wa_low[:, k, :])
        pe.go(lambda e: mm_chain(e, q[:, 0:AW], pairs), done=("A", i))
        act.need(("A", i), ("rrms", i - 1) if i else None)
        act.go(lambda e: e.activation(squares[:, :], q[:, 0:QL], ACT.Square,
                                      accum_out=ssum[:, i, 0:1]), done=("sq", i))
        act.need(("sq", i))
        act.go(lambda e: e.activation(squares[:, 0:KVL], q[:, QL:QL + KVL], ACT.Square,
                                      accum_out=ssum[:, i, 1:2]), done=("sk", i))
        act.need(("sk", i))
        act.go(lambda e: e.activation(rms[:, i, 0:1], ssum[:, i, 0:1], ACT.Sqrt,
                                      bias=eps[:, 1:2], scale=1.0 / QL))
        act.go(lambda e: e.activation(rms[:, i, 1:2], ssum[:, i, 1:2], ACT.Sqrt,
                                      bias=eps[:, 1:2], scale=1.0 / KVL), done=("rms", i))
        dve.need(("rms", i))
        dve.go(lambda e: e.reciprocal(rrms[:, i, :], rms[:, i, :]), done=("rrms", i))
        act.need(("rrms", i))
        if i >= 2:
            act.need(("U", i - 2))
        act.go(lambda e: e.activation(qn[:, r, 0:QL], q[:, 0:QL], ACT.Copy,
                                      scale=rrms[:, i, 0:1]))
        act.go(lambda e: e.activation(qn[:, r, QL:2 * P], q[:, P:QL], ACT.Copy,
                                      scale=rrms[:, i, 0:1]), done=("qn", i))
        j = i % JT
        pe_col = QL + KVL
        dve.need(("qn", i), "kvw", "rk")
        if i >= 2:
            dve.need(("U", i - 2))
        dve.go(lambda e: e.scalar_tensor_tensor(
            out=lat1[:, i, 0:KVL], in0=q[:, QL:pe_col], scalar=rrms[:, i, 1:2],
            in1=kvw_row[:, :], op0=ALU.mult, op1=ALU.mult), done=("lat", i))
        dve.go(lambda e: e.tensor_tensor(kk[:, r, KVL:P], q[:, pe_col:AW], rk[:, j, 0:ROPE],
                                         ALU.mult))
        dve.go(lambda e: e.tensor_tensor(kv2[:, r, 0:HALF], q[:, pe_col + HALF:AW],
                                         rk[:, j, ROPE:ROPE + HALF], ALU.mult))
        dve.go(lambda e: e.tensor_tensor(kv2[:, r, HALF:ROPE], q[:, pe_col:pe_col + HALF],
                                         rk[:, j, ROPE + HALF:2 * ROPE], ALU.mult),
               done=("kk2", i))
        pool.need(("kk2", i), ("lat", i))
        pool.go(lambda e: e.tensor_copy(kk[:, r, 0:KVL], lat1[:, i, 0:KVL]))
        pool.go(lambda e: e.tensor_tensor(kk[:, r, KVL:P], kk[:, r, KVL:P], kv2[:, r, :],
                                          ALU.add), done=("kk", i))

    def transpose_latents(i):
        r = i % 2
        u = u_ps[r]
        tok = slice(i * P, (i + 1) * P)
        pe.need(("qn", i), ("kk", i))
        if i >= 2:
            pe.need(("k low", i - 2))
        def issue(e):
            e.transpose(u[:, 0:P], qn[:, r, 0:P], ident[:, :])
            e.transpose(u[:, P:2 * P], qn[:, r, P:2 * P], ident[:, :])
            return e.transpose(u[:, 2 * P:3 * P], kk[:, r, :], ident[:, :])
        pe.go(issue, done=("U", i))
        act.need(("U", i), "qw")
        act.go(lambda e: e.activation(q_lat["a_high"][:, tok], u[:, 0:P], ACT.Copy,
                                      scale=qw_col[:, 0:1]))
        act.go(lambda e: e.activation(q_lat["b_both"][:, tok], u[:, P:2 * P], ACT.Copy,
                                      scale=qw_col[:, 1:2]))
        act.go(lambda e: e.activation(k_high[:, tok], u[:, 2 * P:3 * P], ACT.Copy),
               done=("high", i))
        dve.need(("high", i))
        dve.go(lambda e: e.scalar_tensor_tensor(
            out=q_lat["a_low"][:, tok], in0=u[:, 0:P], scalar=qw_col[:, 0:1],
            in1=f32(q_lat["a_high"][:, tok]), op0=ALU.mult, op1=ALU.subtract))
        low = q_lat["b_both"][QB:P, tok]
        dve.go(lambda e: e.scalar_tensor_tensor(
            out=low, in0=u[QB:P, P:2 * P], scalar=qw_col[QB:P, 1:2], in1=f32(low),
            op0=ALU.mult, op1=ALU.subtract))
        dve.go(lambda e: e.tensor_tensor(k_low[:, tok], u[:, 2 * P:3 * P], f32(k_high[:, tok]),
                                         ALU.subtract), done=("k low", i))

    normalise(0)
    split_wa()
    for step in range(NT + 2):
        if step + 1 < NT:
            normalise(step + 1)
        if step < NT:
            transpose_x(step)
        if 0 <= step - 1 < NT:
            project(step - 1)
        if 0 <= step - 2 < NT:
            transpose_latents(step - 2)


def fold_weights(core, ctx, sb, pb, wqn, wqp, wk, wv, wo, weff_dram, m_dram):
    pe, act, dve, pool, sync = core.pe, core.act, core.dve, core.pool, core.sync
    FH = 4
    wqn_sb = sb(ctx, "wqn_sb", [P, 2, FH, 2 * P])
    wqp_sb = sb(ctx, "wqp_sb", [P, 2, 2, FH * ROPE])
    wk_sb = sb(ctx, "wk_sb", [P, NH, KVL])
    wv_sb = sb(ctx, "wv_sb", [P, NH, KVL])
    wo_sb = sb(ctx, "wo_sb", [P, 2, FH, DM])
    weff = sb(ctx, "weff_sb", [P, 2, FH, 4, P], F32R)
    m_sb = sb(ctx, "m_sb", [P, 2, FH // 2, 2, DM], F32R)
    f_ps = [pb(ctx, f"f_ps{i}") for i in range(2)]
    sync.load(lambda e: e.dma_start(wk_sb[:, :, :], wk), "wk", core.dma_sem("wk"))
    sync.load(lambda e: e.dma_start(wv_sb[:, :, :], wv), "wv", core.dma_sem("wv"))
    steps = NH // FH
    bank_read = [None, None]
    turn = 0
    for s in range(steps):
        r = s % 2
        heads = slice(s * FH, (s + 1) * FH)
        if s >= 2:
            sync.need(("fold", s - 2), ("rot", s - 2))
        sync.load(lambda e, r=r, heads=heads: e.dma_start(wqn_sb[:, r, :, :], wqn[:, heads, :]),
                  ("wqn", s), core.dma_sem(f"wqn{r}"))
        sync.load(lambda e, r=r, s=s: e.dma_start(
            wqp_sb[:, r, :, :], wqp[:, :, s * FH * ROPE:(s + 1) * FH * ROPE]),
            ("wqp", s), core.dma_sem(f"wqp{r}"))
        if s >= 2:
            sync.need(("M", s - 2, FH // 2 - 1))
        sync.load(lambda e, r=r, heads=heads: e.dma_start(wo_sb[:, r, :, :], wo[:, heads, :]),
                  ("wo", s), core.dma_sem(f"wo{r}"))

        b = turn % 2
        turn += 1
        pe.need(("wqn", s), "wk", bank_read[b])
        f = f_ps[b][:, :].rearrange("p (h c d) -> p h c d", h=FH, c=2)
        def fold(e, r=r, s=s, f=f):
            for h in range(FH):
                for c in range(2):
                    ins = e.matmul(f[:, h, c, :], wqn_sb[:, r, h, c * P:(c + 1) * P],
                                   wk_sb[:, s * FH + h, :], start=True, stop=True)
            return ins
        pe.go(fold, done=("fold", s))
        act.need(("fold", s))
        if s >= 2:
            act.need(("weff out", s - 2))
        act.go(lambda e, r=r, f=f: e.activation(weff[:, r, :, 0::2, 0:KVL], f, ACT.Copy),
               done=("fold high", s))
        dve.need(("fold high", s))
        if s >= 2:
            dve.need(("weff out", s - 2))
        dve.go(lambda e, r=r, f=f: e.tensor_tensor(
            weff[:, r, :, 1::2, 0:KVL], f, f32(weff[:, r, :, 0::2, 0:KVL]), ALU.subtract),
            done=("fold low", s))
        bank_read[b] = ("fold low", s)
        rot = wqp_sb[:, r, :, :].rearrange("p c (h d) -> p h c d", h=FH)
        pool.need(("wqp", s))
        if s >= 2:
            pool.need(("weff out", s - 2))
        pool.go(lambda e, r=r, rot=rot: e.tensor_copy(weff[:, r, :, 0::2, KVL:P], rot),
                done=("rot high", s))
        pool.need(("rot high", s))
        pool.go(lambda e, r=r, rot=rot: e.tensor_tensor(
            weff[:, r, :, 1::2, KVL:P], rot, f32(weff[:, r, :, 0::2, KVL:P]), ALU.subtract),
            done=("rot", s))
        pool.need(("fold low", s), ("rot", s))
        pool.load(lambda e, r=r, heads=heads: e.dma_start(
            f32(weff_dram[heads]).rearrange("h p n -> p h n"),
            f32(weff[:, r, :, :, :]).rearrange("p h c n -> p h (c n)")),
            ("weff out", s), core.dma_sem(f"weffo{r}"))

        for pair in range(FH // 2):
            b = turn % 2
            turn += 1
            pe.need(("wo", s), "wv", bank_read[b])
            def fold_m(e, r=r, s=s, pair=pair, b=b):
                for n in range(2):
                    h = 2 * pair + n
                    ins = e.matmul(f_ps[b][n * KVL:(n + 1) * KVL, :], wv_sb[:, s * FH + h, :],
                                   wo_sb[:, r, h, :], start=True, stop=True)
                return ins
            pe.go(fold_m, done=("M", s, pair))
            act.need(("M", s, pair))
            if s >= 2:
                act.need(("m out", s - 2))
            act.go(lambda e, r=r, pair=pair, b=b: e.activation(
                m_sb[:, r, pair, 0, :], f_ps[b][:, :], ACT.Copy), done=("M high", s, pair))
            dve.need(("M high", s, pair))
            dve.go(lambda e, r=r, pair=pair, b=b: e.tensor_tensor(
                m_sb[:, r, pair, 1, :], f_ps[b][:, :], f32(m_sb[:, r, pair, 0, :]),
                ALU.subtract), done=("M low", s, pair))
            bank_read[b] = ("M low", s, pair)
        per_group = GH // FH
        width = FH // 2 * 2 * DM
        g, part = s // per_group, s % per_group
        pool.need(("M low", s, FH // 2 - 1))
        pool.load(lambda e, r=r, g=g, part=part: e.dma_start(
            f32(m_dram[g][:, part * width:(part + 1) * width]),
            f32(m_sb[:, r, :, :, :]).rearrange("p k c n -> p (k c n)")),
            ("m out", s), core.dma_sem(f"mo{r}"))
    for s in (steps - 2, steps - 1):
        pool.need(("weff out", s), ("m out", s))


def attention(core, ctx, sb, pb, ident, rope_q, far, q_lat, k_high, k_low, lat1, weff_dram,
              m_dram, acc):
    pe, act, dve, pool, sync = core.pe, core.act, core.dve, core.pool, core.sync
    cos_q = sb(ctx, "cos_q", [P, SEQ])
    sin_q = sb(ctx, "sin_q", [P, SEQ])
    far_sb = sb(ctx, "far_sb", [P, SEQ])
    weff = sb(ctx, "weff_in", [P, 2, 4, P], F32R)
    m_in = sb(ctx, "m_in", [P, GK, 2, DM], F32R)
    qf = sb(ctx, "qf", [P, SEQ])
    qs = sb(ctx, "qs", [P, SEQ])
    q_high = sb(ctx, "q_high", [P, 2, SEQ], F32R)
    q_low = sb(ctx, "q_low", [P, 2, SEQ], F32R)
    nbias = sb(ctx, "nbias", [P, 4])
    prob = sb(ctx, "prob", [P, 3, SEQ])
    pt = sb(ctx, "pt", [P, 6, 512])
    rden = sb(ctx, "rden", [P, 2, 4])
    o_n = sb(ctx, "o_n", [P, 2, JT, GH * KVL])
    ot_high = sb(ctx, "ot_high", [P, 2, GK * P], F32R)
    ot_low = sb(ctx, "ot_low", [P, 2, GK * P], F32R)
    s_ps = [pb(ctx, f"s_ps{i}", 1024) for i in range(2)]
    p_ps = [pb(ctx, f"p_ps{i}") for i in range(2)]
    x_ps = pb(ctx, "x_ps")
    o_ps = pb(ctx, "o_ps")
    HW_ = 512

    sync.load(lambda e: e.dma_start(cos_q[:, :], rope_q[0]), "cos_q", core.dma_sem("cosq"))
    sync.load(lambda e: e.dma_start(sin_q[KVL:P, :], rope_q[1][KVL:P, :]), "sin_q",
              core.dma_sem("sinq"))
    sync.load(lambda e: e.dma_start(far_sb[:, :], far), "far", core.dma_sem("far"))

    heads = [(b, h) for b in range(BATCH) for h in range(NH)]
    jobs = [(n, j) for n in range(len(heads)) for j in range(JT)]
    x_read = [None]
    p_turn = [0]
    p_read = [None, None]
    pt_turn = [0]
    pt_slots = {}
    pt_read = [None] * 6

    def queries_load(n):
        if n >= 2:
            sync.need(("Q", n - 2, 1))
        sync.load(lambda e: e.dma_start(
            f32(weff[:, n % 2, :, :]).rearrange("p c n -> p (c n)"),
            f32(weff_dram[heads[n][1]])),
                  ("weff", n), core.dma_sem(f"weff{n % 2}"))

    def queries(n, c):
        b, r = heads[n][0], n % 2
        tok = slice(b * SEQ + c * HW_, b * SEQ + (c + 1) * HW_)
        col = slice(c * HW_, (c + 1) * HW_)
        w = weff[:, r, :, :]
        pe.need(("weff", n), x_read[0])
        pairs = split_passes(w[:, 0, :], w[:, 1, :], q_lat["a_high"][:, tok],
                             q_lat["a_low"][:, tok])
        pairs += [(w[:, 2, :], q_lat["b_both"][:, tok]),
                  (w[0:QB, 3, :], q_lat["b_both"][0:QB, tok])]
        pe.go(lambda e: mm_chain(e, x_ps[:, :], pairs), done=("Q", n, c))
        dve.need(("Q", n, c), "cos_q", "sin_q", ("q split", n - 1, c) if n else None)
        dve.go(lambda e: e.tensor_tensor(qf[:, col], x_ps[:, :], cos_q[:, col], ALU.mult))
        for to, at in ((KVL, KVL + HALF), (KVL + HALF, KVL)):
            last = to != KVL
            dve.go(lambda e, to=to, at=at: e.tensor_tensor(
                qs[to:to + HALF, col], x_ps[at:at + HALF, :], sin_q[at:at + HALF, col],
                ALU.mult), done=("q parts", n, c) if last else None)
        x_read[0] = ("q parts", n, c)
        before = ("q split", n, 0) if c else ("q split", n - 1, 1) if n else None
        pool.need(("q parts", n, c), before)
        pool.go(lambda e: e.tensor_tensor(qf[KVL:P, col], qf[KVL:P, col], qs[KVL:P, col],
                                          ALU.add), done=("q turned", n, c))
        pool.need(("q turned", n, c), ("S", n - 2, JT - 1) if n >= 2 else None)
        pool.go(lambda e: e.tensor_copy(q_high[:, r, col], qf[:, col]), done=("q high", n, c))
        pool.need(("q high", n, c))
        pool.go(lambda e: e.tensor_tensor(q_low[:, r, col], qf[:, col],
                                          f32(q_high[:, r, col]), ALU.subtract),
                done=("q split", n, c))

    def halves(j):
        width = (j + 1) * P
        return [(c, min(HW_, width - c)) for c in range(0, width, HW_)]

    def scores(i):
        n, j = jobs[i]
        b, r = heads[n][0], n % 2
        s = s_ps[i % 2]
        q = slice(j * P, (j + 1) * P)
        pe.need(("q split", n, j * P // HW_), ("exp", i - 2) if i >= 2 else None)
        def issue(e):
            for c, w in halves(j):
                keys = slice(b * SEQ + c, b * SEQ + c + w)
                ins = mm_chain(e, s[:, c:c + w], split_passes(
                    q_high[:, r, q], q_low[:, r, q], k_high[:, keys], k_low[:, keys]))
            return ins
        pe.go(issue, done=("S", n, j))
        width = (j + 1) * P
        dve.need(("S", n, j), "far")
        dve.go(lambda e: e.tensor_tensor_reduce(
            out=s[:, 0:width], in0=s[:, 0:width], in1=far_sb[:, SEQ - width:SEQ], scale=1.0,
            scalar=3e38, op0=ALU.add, op1=ALU.min, accum_out=nbias[:, i % 4:i % 4 + 1]),
            done=("bias", i))

    def exponential(i):
        n, j = jobs[i]
        width = (j + 1) * P
        act.need(("bias", i), ("PT", i - 3) if i >= 3 else None)
        act.go(lambda e: e.activation(prob[:, i % 3, 0:width], s_ps[i % 2][:, 0:width], ACT.Exp,
                                      bias=nbias[:, i % 4:i % 4 + 1], scale=-1.0),
               done=("exp", i))

    def transpose_probs(i):
        n, j = jobs[i]
        pt_slots[i] = []
        for c, w in halves(j):
            bank, slot = p_turn[0] % 2, pt_turn[0] % 6
            p_turn[0] += 1
            pt_turn[0] += 1
            pt_slots[i].append(slot)
            pe.need(("exp", i), p_read[bank])
            def issue(e, c=c, w=w, bank=bank):
                for t in range(0, w, P):
                    ins = e.transpose(p_ps[bank][:, t:t + P],
                                      prob[:, i % 3, c + t:c + t + P], ident[:, :])
                return ins
            last = c + w == (j + 1) * P
            pe.go(issue, done=("PT", i) if last else ("PT", i, c))
            lane = act if c == 0 or j == 5 else dve
            lane.need(("PT", i) if last else ("PT", i, c), pt_read[slot])
            if lane is act:
                lane.go(lambda e, bank=bank, w=w, slot=slot: e.activation(
                    pt[:, slot, 0:w], p_ps[bank][:, 0:w], ACT.Copy), done=("pt", i, c))
            else:
                lane.go(lambda e, bank=bank, w=w, slot=slot: e.tensor_copy(
                    pt[:, slot, 0:w], p_ps[bank][:, 0:w]), done=("pt", i, c))
            p_read[bank] = ("pt", i, c)
            pt_read[slot] = ("PV", i)

    def values(i):
        n, j = jobs[i]
        b, h = heads[n]
        region = j % 4
        pe.need(*[("pt", i, c) for c, _ in halves(j)])
        if i >= 4 and region == 0:
            pe.need(("O", i // 4 - 1))
        def issue(e):
            for t in range(j + 1):
                slot = pt_slots[i][t // 4]
                ins = e.matmul(o_ps[:, region * P:region * P + KVL + 1],
                               pt[:, slot, t % 4 * P:t % 4 * P + P],
                               lat1[:, b * JT + t, :], start=t == 0, stop=t == j)
            return ins
        pe.go(issue, done=("PV", i))
        if region == 3:
            k = i // 4
            g = n // GH
            o = o_ps[:, :].rearrange("p (r n) -> p r n", r=4)
            col = h % GH * KVL
            dve.need(("PV", i))
            dve.go(lambda e: e.reciprocal(rden[:, k % 2, :], o[:, :, KVL]), done=("rden", k))
            dve.need(("rden", k))
            if g >= 2:
                dve.need(("OT", g - 2, JT - 1))
            dve.go(lambda e: e.tensor_tensor(
                o_n[:, g % 2, j - 3:j + 1, col:col + KVL], o[:, :, 0:KVL],
                rden[:, k % 2, :].unsqueeze(2).to_broadcast((P, 4, KVL)), ALU.mult),
                done=("O", k))

    def output_load(g):
        if g >= 1:
            sync.need(("OP", g - 1, JT - 1))
        sync.load(lambda e: e.dma_start(
            f32(m_in[:, :, :, :]).rearrange("p k c n -> p (k c n)"), f32(m_dram[g % NG])), ("m", g), core.dma_sem("m_in"))

    def output_transpose(g, j):
        bank, r = p_turn[0] % 2, j % 2
        p_turn[0] += 1
        last_head = g * GH + GH - 1
        pe.need(("O", (last_head * JT + j) // 4), p_read[bank])
        def issue(e):
            for k in range(GK):
                ins = e.transpose(p_ps[bank][:, k * P:(k + 1) * P],
                                  o_n[:, g % 2, j, k * P:(k + 1) * P], ident[:, :])
            return ins
        pe.go(issue, done=("OT", g, j))
        before = [("OP", g, j - 2)] if j >= 2 else [("OP", g - 1, JT - 2 + j)] if g else []
        act.need(("OT", g, j), *before)
        act.go(lambda e: e.activation(ot_high[:, r, :], p_ps[bank][:, :], ACT.Copy),
               done=("ot high", g, j))
        dve.need(("ot high", g, j))
        dve.go(lambda e: e.tensor_tensor(ot_low[:, r, :], p_ps[bank][:, :],
                                         f32(ot_high[:, r, :]), ALU.subtract),
               done=("ot low", g, j))
        p_read[bank] = ("ot low", g, j)

    def output_project(g, j):
        r, tile = j % 2, g // NG * JT + j
        pe.need(("ot low", g, j), ("m", g), x_read[0])
        pairs = []
        for k in range(GK):
            s = slice(k * P, (k + 1) * P)
            pairs += split_passes(ot_high[:, r, s], ot_low[:, r, s], m_in[:, k, 0, :],
                                  m_in[:, k, 1, :])
        pe.go(lambda e: mm_chain(e, x_ps[:, :], pairs), done=("OP", g, j))
        if g % NG == 0:
            act.need(("OP", g, j))
            act.go(lambda e: e.activation(acc[:, tile, :], x_ps[:, :], ACT.Copy),
                   done=("sum", g, j))
        else:
            dve.need(("OP", g, j), ("sum", g - 1, j))
            dve.go(lambda e: e.tensor_tensor(acc[:, tile, :], x_ps[:, :], acc[:, tile, :],
                                             ALU.add), done=("sum", g, j))
        x_read[0] = ("sum", g, j)

    queries_load(0)
    output_load(0)
    queries_load(1)
    queries(0, 0)
    queries(0, 1)
    group_jobs = GH * JT
    START = 4
    n_groups = len(heads) // GH
    for i in range(len(jobs) + START + 2 * JT + 2):
        if i < len(jobs):
            scores(i)
        if 0 <= i - 2 < len(jobs):
            transpose_probs(i - 2)
        if i < len(jobs):
            exponential(i)
        if 0 <= i - 3 < len(jobs):
            values(i - 3)
        if i < len(jobs):
            n, j = jobs[i]
            if n + 1 < len(heads) and j in (2, 5):
                queries(n + 1, (j - 2) // 3)
                if j == 5 and n + 2 < len(heads):
                    queries_load(n + 2)
        at = i - START
        g, k = at // group_jobs - 1, at % group_jobs
        if 0 <= g < n_groups:
            if k % 2 == 0 and k // 2 < JT:
                output_transpose(g, k // 2)
            elif k % 2 == 1 and k // 2 < JT:
                output_project(g, k // 2)
            elif k == 2 * JT and g + 1 < n_groups:
                output_load(g + 1)


def feed_forward(core, ctx, sb, pb, ident, x_t, x2_dram, acc, wg, wu, wd, sg, su, sd, out_t):
    pe, act, dve, pool, sync = core.pe, core.act, core.dve, core.pool, core.sync
    TT = TB // P
    xt_high = sb(ctx, "ft_high", [P, KD, TOKENS], F32R)
    xt_low = sb(ctx, "ft_low", [P, KD, TOKENS], F32R)
    raw = sb(ctx, "w_raw", [P, 3, KD * FG * P], I32)
    w_high = sb(ctx, "w_high", [P, 2, 3, KD * FG * P], F32R)
    w_low = sb(ctx, "w_low", [P, 2, 3, KD * FG * P], F32R)
    scale = sb(ctx, "scale", [P, 3])
    xin = sb(ctx, "f_xin", [P, 2, DM])
    tmp = sb(ctx, "f_tmp", [P, 2, DM])
    stats = sb(ctx, "f_stats", [P, 3, NT, 6])
    mv = sb(ctx, "f_mv", [P, 3, NT, 2])
    dev = sb(ctx, "f_dev", [P, 3, NT])
    rstd = sb(ctx, "f_rstd", [P, 3, NT])
    gate = sb(ctx, "gate", [P, 2, TB])
    mid = sb(ctx, "mid", [P, 2, TB])
    mid_high = sb(ctx, "mid_high", [P, 2, FG, TB], F32R)
    mid_low = sb(ctx, "mid_low", [P, 2, FG, TB], F32R)
    eps = sb(ctx, "eps2", [P, 1])
    t_ps = [pb(ctx, f"ft_ps{i}") for i in range(2)]
    g_ps = [pb(ctx, f"fg_ps{i}") for i in range(2)]
    u_ps = [pb(ctx, f"fu_ps{i}") for i in range(2)]
    d_ps = [pb(ctx, f"fd_ps{i}") for i in range(2)]
    dve.go(lambda e: e.memset(eps[:, :], LN_EPS), done="eps2")
    for n, s in enumerate((sg, su, sd)):
        sync.load(lambda e, n=n, s=s: e.dma_start(scale[:, n:n + 1], s.to_broadcast((P, 1))),
                  ("scale", n), core.dma_sem(f"scale{n}"))

    def hidden(g):
        return g * FG * P, min(FG * P, HID - g * FG * P)

    def weight_views(t, g, n):
        h0, hw = hidden(g)
        if n < 2:
            return t[:, 0:KD * hw].rearrange("p (k h) -> p k h", k=KD)
        return t[:, 0:FG * DM].rearrange("p (k m) -> p k m", k=FG)

    def weights(g):
        h0, hw = hidden(g)
        r = g % 2
        for n, w in enumerate((wg, wu, wd)):
            if g >= 1:
                sync.need(("w low", g - 1, n))
            dst = weight_views(raw[:, n, :], g, n)
            parts = []
            if n < 2:
                src = w[:, h0:h0 + hw].rearrange("(k p) h -> p k h", p=P)
                sync.load(lambda e, dst=dst, src=src: e.dma_start(dst, src), ("w", g, n),
                          core.dma_sem(f"w_raw{n}"))
                parts.append((P, slice(0, KD * hw)))
            else:
                for k in range(-(-hw // P)):
                    rows = min(P, hw - k * P)
                    src = w[h0 + k * P:h0 + k * P + rows, :]
                    sync.load(lambda e, dst=dst, src=src, k=k, rows=rows: e.dma_start(
                        dst[0:rows, k, :], src), ("w", g, n, k), core.dma_sem(f"w_raw{n}{k}"))
                    parts.append((rows, slice(k * DM, (k + 1) * DM)))
            for k, (rows, s) in enumerate(parts):
                act.need(("w", g, n) if n < 2 else ("w", g, n, k), ("scale", n),
                         ("D", g - 2, NTB - 1) if g >= 2 else None)
                act.go(lambda e, n=n, rows=rows, s=s: e.activation(
                    w_high[0:rows, r, n, s], raw[0:rows, n, s], ACT.Copy,
                    scale=scale[0:rows, n:n + 1]), done=("w high", g, n, k))
                dve.need(("w high", g, n, k))
                dve.go(lambda e, n=n, rows=rows, s=s: e.scalar_tensor_tensor(
                    out=w_low[0:rows, r, n, s], in0=raw[0:rows, n, s],
                    scalar=scale[0:rows, n:n + 1], in1=f32(w_high[0:rows, r, n, s]),
                    op0=ALU.mult, op1=ALU.subtract),
                    done=("w low", g, n) if k == len(parts) - 1 else None)

    def norm_stats(which, tb, source, ready):
        tiles = range(tb * TT, (tb + 1) * TT)
        for i in tiles:
            dve.need(*ready(i))
            dve.go(lambda e, i=i: e.bn_stats(stats[:, which, i, :], source(i)),
                   done=("fst", which, i))
        for i in tiles:
            dve.need(("fst", which, i))
            dve.go(lambda e, i=i: e.bn_aggr(mv[:, which, i, :], stats[:, which, i, :]),
                   done=("fmv", which, i))
        t = slice(tb * TT, (tb + 1) * TT)
        act.need(("fmv", which, tiles[-1]), "eps2")
        act.go(lambda e: e.activation(dev[:, which, t], mv[:, which, t, 1], ACT.Sqrt,
                                      bias=eps[:, :]), done=("fdev", which, tb))
        dve.need(("fdev", which, tb))
        dve.go(lambda e: e.reciprocal(rstd[:, which, t], dev[:, which, t]),
               done=("frstd", which, tb))

    def apply_norm(which, i, dst, src, done):
        dve.need(("frstd", which, i // TT))
        dve.go(lambda e: e.tensor_scalar(dst, src, mv[:, which, i, 0:1],
                                         rstd[:, which, i:i + 1], ALU.subtract, ALU.mult),
               done=done)

    def prepare(tb):
        tiles = range(tb * TT, (tb + 1) * TT)
        norm_stats(0, tb, lambda i: acc[:, i, :], lambda i: [])
        for i in tiles:
            r = i % 2
            if i >= 2:
                sync.need(("x2", i - 2))
            sync.load(lambda e, i=i, r=r: e.dma_start(xin[:, r, :], x_t[i]), ("fx", i),
                      core.dma_sem(f"fx{r}"))
            apply_norm(0, i, acc[:, i, :], acc[:, i, :], ("n0", i))
            dve.need(("n0", i), ("fx", i))
            dve.go(lambda e, i=i, r=r: e.tensor_tensor(acc[:, i, :], acc[:, i, :],
                                                       xin[:, r, :], ALU.add),
                   done=("x2", i))
            if i >= 2:
                pool.need(("x2 out", i - 2))
            pool.need(("x2", i))
            pool.load(lambda e, i=i: e.dma_start(x2_dram[i], acc[:, i, :]), ("x2 out", i),
                      core.dma_sem(f"x2o{r}"))
        norm_stats(1, tb, lambda i: acc[:, i, :], lambda i: [("x2", i)])
        for i in tiles:
            r = i % 2
            if i >= 2:
                dve.need(("FT", i - 2))
            apply_norm(1, i, tmp[:, r, :], acc[:, i, :], ("xf", i))
            pe.need(("xf", i), ("ft low", i - 2) if i >= 2 else None)
            def issue(e, i=i, r=r):
                for k in range(KD):
                    ins = e.transpose(t_ps[r][:, k * P:(k + 1) * P],
                                      tmp[:, r, k * P:(k + 1) * P], ident[:, :])
                return ins
            pe.go(issue, done=("FT", i))
            tok = slice(i * P, (i + 1) * P)
            view = t_ps[r][:, :].rearrange("p (k t) -> p k t", k=KD)
            act.need(("FT", i))
            act.go(lambda e, tok=tok, view=view: e.activation(xt_high[:, :, tok], view,
                                                              ACT.Copy), done=("ft high", i))
            dve.need(("ft high", i))
            dve.go(lambda e, tok=tok, view=view: e.tensor_tensor(
                xt_low[:, :, tok], view, f32(xt_high[:, :, tok]), ALU.subtract),
                done=("ft low", i))

    unit = [0]
    unit_of = {}

    def gate_up(g, tb):
        h0, hw = hidden(g)
        r, m = g % 2, (g * NTB + tb) % 2
        tok = slice(tb * TB, (tb + 1) * TB)
        for k in range(-(-hw // P)):
            rows = min(P, hw - k * P)
            n = unit[0]
            unit[0] += 1
            b = n % 2
            pe.need(("ft low", (tb + 1) * TT - 1), ("w low", g, 0), ("w low", g, 1),
                    ("mid", n - 2) if n >= 2 else None)
            for which, bank in ((0, g_ps[b]), (1, u_ps[b])):
                wh = weight_views(w_high[:, r, which, :], g, which)
                wl = weight_views(w_low[:, r, which, :], g, which)
                cols = slice(k * P, k * P + rows)
                pairs = []
                for d in range(KD):
                    pairs += split_passes(wh[:, d, cols], wl[:, d, cols], xt_high[:, d, tok],
                                          xt_low[:, d, tok])
                pe.go(lambda e, bank=bank, rows=rows, pairs=pairs: mm_chain(
                    e, bank[0:rows, :], pairs), done=("gu", n, which))
            act.need(("gu", n, 0), ("mid", n - 2) if n >= 2 else None)
            act.go(lambda e, b=b, rows=rows: e.activation(
                gate[0:rows, b, :], g_ps[b][0:rows, :], ACT.Silu), done=("silu", n))
            dve.need(("silu", n), ("gu", n, 1), ("mid low", n - 2) if n >= 2 else None)
            dve.go(lambda e, b=b, rows=rows: e.tensor_tensor(
                mid[0:rows, b, :], u_ps[b][0:rows, :], gate[0:rows, b, :], ALU.mult),
                done=("mid", n))
            before = g * NTB + tb - 2
            act.need(("mid", n), ("D", before // NTB, before % NTB) if before >= 0 else None)
            act.go(lambda e, b=b, rows=rows, k=k, m=m: e.activation(
                mid_high[0:rows, m, k, :], mid[0:rows, b, :], ACT.Copy), done=("mid high", n))
            pool.need(("mid high", n))
            pool.go(lambda e, b=b, rows=rows, k=k, m=m: e.tensor_tensor(
                mid_low[0:rows, m, k, :], mid[0:rows, b, :],
                f32(mid_high[0:rows, m, k, :]), ALU.subtract), done=("mid low", n))
            unit_of[g, tb] = n

    down_turn = [0]
    d_read = [None, None]

    def down(g, tb):
        h0, hw = hidden(g)
        r, m = g % 2, (g * NTB + tb) % 2
        wh = weight_views(w_high[:, r, 2, :], g, 2)
        wl = weight_views(w_low[:, r, 2, :], g, 2)
        for t in range(TT):
            i = tb * TT + t
            b = down_turn[0] % 2
            down_turn[0] += 1
            pe.need(("mid low", unit_of[g, tb]), ("w low", g, 2), d_read[b])
            pairs = []
            for k in range(-(-hw // P)):
                rows = min(P, hw - k * P)
                s = slice(t * P, (t + 1) * P)
                pairs += split_passes(mid_high[0:rows, m, k, s], mid_low[0:rows, m, k, s],
                                      wh[0:rows, k, :], wl[0:rows, k, :])
            last = t == TT - 1
            name = ("D", g, tb) if last else ("D", g, tb, t)
            pe.go(lambda e, b=b, pairs=pairs: mm_chain(e, d_ps[b][:, :], pairs), done=name)
            if g == 0:
                act.need(name, ("x2 out", i), ("xf", i))
                act.go(lambda e, b=b, i=i: e.activation(acc[:, i, :], d_ps[b][:, :], ACT.Copy),
                       done=("part", g, i))
            else:
                dve.need(name, ("part", g - 1, i))
                dve.go(lambda e, b=b, i=i: e.tensor_tensor(
                    acc[:, i, :], d_ps[b][:, :], acc[:, i, :], ALU.add), done=("part", g, i))
            d_read[b] = ("part", g, i)

    def finish(tb):
        norm_stats(2, tb, lambda i: acc[:, i, :], lambda i: [("part", NFG - 1, i)])
        for i in range(tb * TT, (tb + 1) * TT):
            r = i % 2
            sync.need(("y", i - 2) if i >= 2 else ("x2", NT - 2 + i))
            sync.load(lambda e, i=i, r=r: e.dma_start(xin[:, r, :], x2_dram[i]), ("fx2", i),
                      core.dma_sem(f"fx{r}"))
            apply_norm(2, i, acc[:, i, :], acc[:, i, :], ("n2", i))
            pool.need(("n2", i), ("fx2", i))
            pool.go(lambda e, i=i, r=r: e.tensor_tensor(acc[:, i, :], acc[:, i, :],
                                                        xin[:, r, :], ALU.add),
                    done=("y", i))
            sync.need(("y", i))
            sync.load(lambda e, i=i: e.dma_start(out_t[i], acc[:, i, :]), ("out", i),
                      core.dma_sem(f"out{i}"))

    prepare(0)
    weights(0)
    blocks = [(g, tb) for g in range(NFG) for tb in range(NTB)]
    for n in range(len(blocks) + 1):
        if n < len(blocks):
            g, tb = blocks[n]
            gate_up(g, tb)
            if g == 0 and tb + 1 < NTB:
                prepare(tb + 1)
        if n >= 1:
            g, tb = blocks[n - 1]
            down(g, tb)
            if tb == 0 and g + 1 < NFG:
                weights(g + 1)
            if g == NFG - 1:
                finish(tb)
    for i in range(NT):
        sync.need(("out", i))


def _tables():
    import numpy as np
    exponents = np.arange(0, ROPE, 2, dtype=np.float32) / np.float32(ROPE)
    freqs = np.float32(1.0) / np.power(np.float32(10000.0), exponents)
    angles = np.outer(np.arange(SEQ, dtype=np.float32), freqs.astype(np.float32))
    cos, sin = np.cos(angles), np.sin(angles)
    rope_k = np.concatenate([cos, cos, -sin, sin], axis=1).astype(np.float32)
    scale = -1.0 / np.sqrt(np.float64(NOPE + ROPE))
    rope_q = np.zeros((2, P, SEQ), np.float32)
    rope_q[0, 0:KVL] = scale
    rope_q[0, KVL:P] = np.concatenate([cos.T, cos.T]) * scale
    rope_q[1, KVL:P] = np.concatenate([sin.T, -sin.T]) * scale
    far = np.zeros((P, SEQ), np.float32)
    far[:, SEQ - P:] = np.where(np.arange(P)[None, :] > np.arange(P)[:, None], FAR, 0.0)
    return rope_k, rope_q, far


def kernel(**inputs):
    import numpy as np
    import concourse.bacc as bacc
    from concourse.bass_utils import run_bass_kernel_spmd

    get = lambda n: np.asarray(inputs[n])
    evens_odds = lambda a: np.concatenate([a[..., 0::2, :], a[..., 1::2, :]], axis=-2)
    wkv_a = get("L0_attn_wkv_a")
    wq_b = get("L0_attn_wq_b").reshape(NH, NOPE + ROPE, QL)
    wkv_b = get("L0_attn_wkv_b").reshape(NH, NOPE + VD, KVL)
    wa = np.concatenate([get("L0_attn_wq_a"), wkv_a[:KVL], evens_odds(wkv_a[KVL:])], axis=0).T
    twice = lambda a: np.concatenate([a, a[..., P:QL]], axis=-1)
    wqn = twice(wq_b[:, :NOPE]).transpose(1, 0, 2)
    wqp = twice(evens_odds(wq_b[:, NOPE:])).reshape(NH * ROPE, 2, P).transpose(2, 1, 0)
    rope_k, rope_q, far = _tables()
    arrays = {
        "x": get("L0_attn_x").reshape(TOKENS, DM),
        "wa": wa, "wqn": wqn, "wqp": wqp,
        "wk": wkv_b[:, :NOPE].transpose(1, 0, 2),
        "wv": wkv_b[:, NOPE:].transpose(1, 0, 2),
        "wo": get("L0_attn_wo").T.reshape(NH, VD, DM).transpose(1, 0, 2),
        "qw": twice(get("L0_attn_q_norm_w")).reshape(2, P).T,
        "kvw": get("L0_attn_kv_norm_w").reshape(1, KVL),
        "rope_k": rope_k, "rope_q": rope_q, "far": far,
        "wg": get("L0_ffn_w_gate").T, "wu": get("L0_ffn_w_up").T, "wd": get("L0_ffn_w_down").T,
        "sg": get("L0_ffn_scale_gate").reshape(1, 1),
        "su": get("L0_ffn_scale_up").reshape(1, 1),
        "sd": get("L0_ffn_scale_down").reshape(1, 1),
    }
    arrays = {n: np.ascontiguousarray(a) for n, a in arrays.items()}
    nc = bacc.Bacc("TRN2", target_bir_lowering=False, num_devices=1)
    args = [nc.dram_tensor(n, a.shape, mybir.dt.from_np(a.dtype), kind="ExternalInput").ap()
            for n, a in arrays.items()]
    out = nc.dram_tensor("out", (TOKENS, DM), F32, kind="ExternalOutput").ap()
    layer_kernel(nc, *args, out)
    result = run_bass_kernel_spmd(nc, [arrays], core_ids=[0])
    return result.results[0]["out"].reshape(BATCH, SEQ, DM)
```

```python
import concourse.bass as bass
from concourse import mybir
from contextlib import ExitStack

F32 = mybir.dt.float32
F32R = mybir.dt.float32r
I32 = mybir.dt.int32
ALU = mybir.AluOpType
ACT = mybir.ActivationFunctionType

P = 128
BATCH, SEQ, DM = 2, 1024, 512
TOKENS = BATCH * SEQ
NT = TOKENS // P
JT = SEQ // P
KD = DM // P
NH, NOPE, ROPE, VD = 32, 128, 64, 128
QL, KVL = 192, 64
HALF = ROPE // 2
QB = QL - P
AW = QL + KVL + ROPE
GH = 4
NG = NH // GH
GK = GH * KVL // P
HID = 1376
HT = -(-HID // P)
FG = 2
NFG = -(-HT // FG)
TB = 512
NTB = TOKENS // TB
FH = 4
LAG = 3
UNITS = (0, 1, 2, 3)
Q_STEPS = (2, 6)
Q_SPLIT = 3
O_STEPS = (4, 7)
M_STEP = 3
LN_EPS, RMS_EPS = 1e-5, 1e-6
FAR = 1e38


class Lane:

    def __init__(self, reached, sem=None):
        self.reached, self.sem, self.count, self.steps = reached, sem, 0, []
        self.passed = {}

    def need(self, *names):
        for n in names:
            if n is not None:
                assert n in self.reached, n
                self.steps.append(("need", n))

    def go(self, issue, done=None):
        if done is not None:
            assert done not in self.reached, done
            self.count += 1
            self.reached[done] = (self.sem, self.count)
        self.steps.append(("go", issue, self.sem if done is not None else None, 1))

    def load(self, issue, done, sem):
        assert done not in self.reached, done
        n = sem.count = sem.count + 16
        self.reached[done] = (sem, n)
        self.steps.append(("go", issue, sem, 16))

    def play(self, eng):
        for kind, what, *inc in self.steps:
            if kind == "need":
                sem, value = self.reached[what]
                if self.passed.get(sem.name, 0) < value:
                    self.passed[sem.name] = value
                    eng.wait_ge(sem.handle, value)
            else:
                ins = what(eng)
                if inc[0] is not None:
                    ins.then_inc(inc[0].handle, inc[1])
        self.steps = []


class Sem:
    def __init__(self, ctx, nc, name):
        self.name, self.count = name, 0
        self.handle = ctx.enter_context(nc.semaphore(name))


class Core:

    def __init__(self, ctx, nc):
        self.ctx, self.nc, self.reached, self.sems = ctx, nc, {}, {}
        self.pe, self.act, self.dve, self.pool = (
            Lane(self.reached, Sem(ctx, nc, f"s_{n}")) for n in ("pe", "act", "dve", "pool"))
        self.sync = Lane(self.reached)

    def dma_sem(self, name):
        if name not in self.sems:
            self.sems[name] = Sem(self.ctx, self.nc, f"s_{name}")
        return self.sems[name]

    def play(self):
        with self.nc.Block() as block:
            block.sync(self.sync.play)
            block.tensor(self.pe.play)
            block.vector(self.dve.play)
            block.scalar(self.act.play)
            block.gpsimd(self.pool.play)


def f32(ap):
    return ap.bitcast(F32)


def split_passes(a_high, a_low, b_high, b_low):
    return [(a_high, b_high), (a_high, b_low), (a_low, b_high)]


def mm_chain(eng, out, pairs):
    for n, (stationary, moving) in enumerate(pairs):
        ins = eng.matmul(out, stationary, moving, start=n == 0, stop=n == len(pairs) - 1)
    return ins


def layer_kernel(nc, x, wa, wqn, wqp, wk, wv, wo, qw, kvw, rope_k, rope_q, far, wg, wu, wd,
                 sg, su, sd, out):
    weff_dram = nc.dram_tensor("weff", (NH, P, 4 * P), F32R, kind="Internal").ap()
    m_dram = nc.dram_tensor("m_fold", (NG, P, GK * 2 * DM), F32R, kind="Internal").ap()
    attn_dram = nc.dram_tensor("attn_out", (NT, P, DM), F32, kind="Internal").ap()
    x2_dram = nc.dram_tensor("x_mid", (NT, P, DM), F32, kind="Internal").ap()
    x_t = x.rearrange("(n p) d -> n p d", p=P)
    out_t = out.rearrange("(n p) d -> n p d", p=P)

    with ExitStack() as whole:
        core = Core(whole, nc)

        def sb(ctx, name, shape, dt=F32):
            return ctx.enter_context(nc.sbuf_tensor(name, shape, dt))

        def pb(ctx, name, width=512):
            return ctx.enter_context(nc.psum_tensor(name, [P, width], F32))

        ident = sb(whole, "ident", [P, P])
        core.pool.go(lambda e: e.memset(ident[:, :], 0.0), done="ident zero")
        core.pool.need("ident zero")
        core.pool.go(lambda e: e.affine_select(
            out=ident[:, :], in_=ident[:, :], compare_op=ALU.not_equal, fill=1.0, base=0,
            pattern=[[-1, P]], channel_multiplier=1), done="ident")

        with ExitStack() as attn:
            q_lat = {
                "a_high": sb(attn, "qa_high", [P, TOKENS], F32R),
                "a_low": sb(attn, "qa_low", [P, TOKENS], F32R),
                "b_both": sb(attn, "qb_both", [P, TOKENS], F32R),
            }
            k_high = sb(attn, "k_high", [P, TOKENS], F32R)
            k_low = sb(attn, "k_low", [P, TOKENS], F32R)
            lat2 = sb(attn, "lat2", [P, NT, P], F32R)
            with ExitStack() as ctx:
                prologue(core, ctx, sb, pb, ident, x_t, wa, qw, kvw, rope_k, q_lat, k_high,
                         k_low, lat2, wqn, wqp, wk, weff_dram)
                core.play()
            with ExitStack() as ctx:
                attention(core, ctx, sb, pb, ident, rope_q, far, q_lat, k_high, k_low, lat2,
                          weff_dram, m_dram, wv, wo, attn_dram)
                core.play()
        with ExitStack() as ctx:
            feed_forward(core, ctx, sb, pb, ident, x_t, x2_dram, attn_dram, wg, wu, wd, sg, su,
                         sd, out_t)
            core.play()


def latents(core, ctx, sb, pb, ident, x_t, wa, qw, kvw, rope_k, q_lat, k_high, k_low, lat2):
    pe, act, dve, pool, sync = core.pe, core.act, core.dve, core.pool, core.sync
    NX, NA = 4, 3
    wa_raw = sb(ctx, "wa_raw", [P, KD, AW])
    wa_high = sb(ctx, "wa_high", [P, KD, AW], F32R)
    wa_low = sb(ctx, "wa_low", [P, KD, AW], F32R)
    qw_col = sb(ctx, "qw_col", [P, 2])
    kvw_row = sb(ctx, "kvw_row", [P, KVL])
    rk = sb(ctx, "rope_k_sb", [P, JT, 4 * HALF])
    xin = sb(ctx, "xin", [P, NX, DM])
    stats = sb(ctx, "stats", [P, NT, 6])
    mv = sb(ctx, "mv", [P, NT, 2])
    dev = sb(ctx, "dev", [P, NT])
    rstd = sb(ctx, "rstd", [P, NT])
    xn = sb(ctx, "xn", [P, 2, DM])
    xt_high = sb(ctx, "xt_high", [P, 2, DM], F32R)
    xt_low = sb(ctx, "xt_low", [P, 2, DM], F32R)
    squares = sb(ctx, "squares", [P, 2, QL])
    ssum = sb(ctx, "ssum", [P, NT, 2])
    rms = sb(ctx, "rms", [P, NT, 2])
    rrms = sb(ctx, "rrms", [P, NT, 2])
    qn = sb(ctx, "qn", [P, 2, 2 * P])
    kk = sb(ctx, "kk", [P, 2, P])
    kv2 = sb(ctx, "kv2", [P, 2, ROPE])
    t_ps = [pb(ctx, f"t_ps{i}") for i in range(2)]
    a_ps = [pb(ctx, f"a_ps{i}") for i in range(NA)]
    u_ps = [pb(ctx, f"u_ps{i}") for i in range(2)]
    eps = sb(ctx, "eps1", [P, 2])
    dve.go(lambda e: e.memset(eps[:, 0:1], LN_EPS))
    dve.go(lambda e: e.memset(eps[:, 1:2], RMS_EPS), done="eps1")

    def load_x(i):
        if i >= NX:
            sync.need(("xn", i - NX))
        sync.load(lambda e: e.dma_start(xin[:, i % NX, :], x_t[i]), ("x", i),
                  core.dma_sem(f"x{i % NX}"))

    load_x(0)
    load_x(1)
    sync.load(lambda e: e.dma_start(wa_raw[:, :, :], wa.rearrange("(k p) n -> p k n", p=P)),
              "wa", core.dma_sem("wa"))
    load_x(2)
    for name, dst, src in (("qw", qw_col[:, :], qw),
                           ("kvw", kvw_row[:, :], kvw.to_broadcast((P, KVL))),
                           ("rk", rk[:, :, :], rope_k.rearrange("(j p) n -> p j n", p=P))):
        sync.load(lambda e, dst=dst, src=src: e.dma_start(dst, src), name, core.dma_sem(name))

    def split_wa():
        act.need("wa")
        act.go(lambda e: e.activation(wa_high[:, :, :], wa_raw[:, :, :], ACT.Copy), done="wa high")
        dve.need("wa high")
        dve.go(lambda e: e.tensor_tensor(wa_low[:, :, :], wa_raw[:, :, :], f32(wa_high[:, :, :]),
                                         ALU.subtract), done="wa low")

    def statistics(i):
        if i + 1 < NT and i >= 2:
            load_x(i + 1)
        dve.need(("x", i))
        dve.go(lambda e: e.bn_stats(stats[:, i, :], xin[:, i % NX, :]), done=("st", i))
        dve.need(("st", i))
        dve.go(lambda e: e.bn_aggr(mv[:, i, :], stats[:, i, :]), done=("mv", i))
        act.need(("mv", i), "eps1")
        act.go(lambda e: e.activation(dev[:, i:i + 1], mv[:, i, 1:2], ACT.Sqrt,
                                      bias=eps[:, 0:1]), done=("dev", i))

    def normalise(i):
        dve.need(("dev", i))
        dve.go(lambda e: e.reciprocal(rstd[:, i:i + 1], dev[:, i:i + 1]), done=("rstd", i))
        dve.need(("rstd", i))
        if i >= 2:
            dve.need(("T", i - 2))
        dve.go(lambda e: e.tensor_scalar(xn[:, i % 2, :], xin[:, i % NX, :], mv[:, i, 0:1],
                                         rstd[:, i:i + 1], ALU.subtract, ALU.mult),
               done=("xn", i))

    def transpose_x(i):
        r = i % 2
        pe.need(("xn", i), "ident")
        if i >= 2:
            pe.need(("xt low", i - 2))
        def issue(e):
            for k in range(KD):
                ins = e.transpose(t_ps[r][:, k * P:(k + 1) * P], xn[:, r, k * P:(k + 1) * P],
                                  ident[:, :])
            return ins
        pe.go(issue, done=("T", i))
        act.need(("T", i))
        if i >= 2:
            act.need(("A", i - 2))
        act.go(lambda e: e.activation(xt_high[:, r, :], t_ps[r][:, :], ACT.Copy),
               done=("xt high", i))
        dve.need(("xt high", i))
        dve.go(lambda e: e.tensor_tensor(xt_low[:, r, :], t_ps[r][:, :], f32(xt_high[:, r, :]),
                                         ALU.subtract), done=("xt low", i))

    def project(i):
        r = i % 2
        q = a_ps[i % NA]
        pe.need(("xt low", i), "wa low")
        if i >= NA:
            pe.need(("qn", i - NA))
        pairs = []
        for k in range(KD):
            s = slice(k * P, (k + 1) * P)
            pairs += split_passes(xt_high[:, r, s], xt_low[:, r, s], wa_high[:, k, :],
                                  wa_low[:, k, :])
        pe.go(lambda e: mm_chain(e, q[:, 0:AW], pairs), done=("A", i))
        act.need(("A", i), ("sk", i - 1) if i else None)
        act.go(lambda e: e.activation(squares[:, 0, :], q[:, 0:QL], ACT.Square,
                                      accum_out=ssum[:, i, 0:1]))
        act.go(lambda e: e.activation(squares[:, 1, 0:KVL], q[:, QL:QL + KVL], ACT.Square,
                                      accum_out=ssum[:, i, 1:2]), done=("sk", i))
        act.need(("sk", i))
        act.go(lambda e: e.activation(rms[:, i, 0:1], ssum[:, i, 0:1], ACT.Sqrt,
                                      bias=eps[:, 1:2], scale=1.0 / QL))
        act.go(lambda e: e.activation(rms[:, i, 1:2], ssum[:, i, 1:2], ACT.Sqrt,
                                      bias=eps[:, 1:2], scale=1.0 / KVL), done=("rms", i))

    def norm_latents(i):
        r, j = i % 2, i % JT
        q = a_ps[i % NA]
        pe_col = QL + KVL
        dve.need(("rms", i), "kvw", "rk")
        dve.go(lambda e: e.reciprocal(rrms[:, i, :], rms[:, i, :]), done=("rrms", i))
        dve.need(("rrms", i))
        if i >= 2:
            dve.need(("U", i - 2))
        dve.go(lambda e: e.scalar_tensor_tensor(
            out=kk[:, r, 0:KVL], in0=q[:, QL:pe_col], scalar=rrms[:, i, 1:2],
            in1=kvw_row[:, :], op0=ALU.mult, op1=ALU.mult))
        dve.go(lambda e: e.tensor_tensor(kk[:, r, KVL:P], q[:, pe_col:AW], rk[:, j, 0:ROPE],
                                         ALU.mult))
        dve.go(lambda e: e.tensor_tensor(kv2[:, r, 0:HALF], q[:, pe_col + HALF:AW],
                                         rk[:, j, ROPE:ROPE + HALF], ALU.mult))
        dve.go(lambda e: e.tensor_tensor(kv2[:, r, HALF:ROPE], q[:, pe_col:pe_col + HALF],
                                         rk[:, j, ROPE + HALF:2 * ROPE], ALU.mult),
               done=("kk2", i))
        act.need(("kk2", i))
        act.go(lambda e: e.activation(qn[:, r, 0:QL], q[:, 0:QL], ACT.Copy,
                                      scale=rrms[:, i, 0:1]))
        act.go(lambda e: e.activation(qn[:, r, QL:2 * P], q[:, P:QL], ACT.Copy,
                                      scale=rrms[:, i, 0:1]), done=("qn", i))
        pool.need(("kk2", i))
        pool.go(lambda e: e.tensor_tensor(kk[:, r, KVL:P], kk[:, r, KVL:P], kv2[:, r, :],
                                          ALU.add), done=("kk", i))
        pool.go(lambda e: e.tensor_copy(lat2[:, i, 0:KVL], kk[:, r, 0:KVL]), done=("lat high", i))
        pool.need(("lat high", i))
        pool.go(lambda e: e.tensor_tensor(lat2[:, i, KVL:P], kk[:, r, 0:KVL],
                                          f32(lat2[:, i, 0:KVL]), ALU.subtract),
                done=("lat", i))

    def transpose_latents(i):
        r = i % 2
        u = u_ps[r]
        tok = slice(i * P, (i + 1) * P)
        pe.need(("qn", i), ("lat", i))
        if i >= 2:
            pe.need(("k low", i - 2))
        def issue(e):
            e.transpose(u[:, 0:P], qn[:, r, 0:P], ident[:, :])
            e.transpose(u[:, P:2 * P], qn[:, r, P:2 * P], ident[:, :])
            return e.transpose(u[:, 2 * P:3 * P], kk[:, r, :], ident[:, :])
        pe.go(issue, done=("U", i))
        act.need(("U", i), "qw")
        act.go(lambda e: e.activation(q_lat["a_high"][:, tok], u[:, 0:P], ACT.Copy,
                                      scale=qw_col[:, 0:1]))
        act.go(lambda e: e.activation(q_lat["b_both"][:, tok], u[:, P:2 * P], ACT.Copy,
                                      scale=qw_col[:, 1:2]))
        act.go(lambda e: e.activation(k_high[:, tok], u[:, 2 * P:3 * P], ACT.Copy),
               done=("high", i))
        dve.need(("high", i))
        dve.go(lambda e: e.scalar_tensor_tensor(
            out=q_lat["a_low"][:, tok], in0=u[:, 0:P], scalar=qw_col[:, 0:1],
            in1=f32(q_lat["a_high"][:, tok]), op0=ALU.mult, op1=ALU.subtract))
        low = q_lat["b_both"][QB:P, tok]
        dve.go(lambda e: e.scalar_tensor_tensor(
            out=low, in0=u[QB:P, P:2 * P], scalar=qw_col[QB:P, 1:2], in1=f32(low),
            op0=ALU.mult, op1=ALU.subtract))
        dve.go(lambda e: e.tensor_tensor(k_low[:, tok], u[:, 2 * P:3 * P], f32(k_high[:, tok]),
                                         ALU.subtract), done=("k low", i))

    split_wa()
    return [statistics, normalise, transpose_x, project, norm_latents, transpose_latents]


def fold_queries(core, ctx, sb, pb, wqn, wqp, wk, weff_dram):
    pe, act, dve, pool, sync = core.pe, core.act, core.dve, core.pool, core.sync
    wqn_sb = sb(ctx, "wqn_sb", [P, 2, FH, 2 * P])
    wqp_sb = sb(ctx, "wqp_sb", [P, 2, 2, FH * ROPE])
    wk_sb = sb(ctx, "wk_sb", [P, NH, KVL])
    weff = sb(ctx, "weff_sb", [P, 2, FH, 4, P], F32R)
    f_ps = pb(ctx, "f_ps")

    def load(s):
        r = s % 2
        heads = slice(s * FH, (s + 1) * FH)
        if s == 0:
            sync.load(lambda e: e.dma_start(wk_sb[:, :, :], wk), "wk", core.dma_sem("wk"))
        if s >= 2:
            sync.need(("fold", s - 2), ("rot", s - 2))
        sync.load(lambda e: e.dma_start(wqn_sb[:, r, :, :], wqn[:, heads, :]),
                  ("wqn", s), core.dma_sem(f"wqn{r}"))
        sync.load(lambda e: e.dma_start(
            wqp_sb[:, r, :, :], wqp[:, :, s * FH * ROPE:(s + 1) * FH * ROPE]),
            ("wqp", s), core.dma_sem(f"wqp{r}"))

    def fold(s):
        r = s % 2
        heads = slice(s * FH, (s + 1) * FH)
        free = ("weff out", s - 2) if s >= 2 else None
        pe.need(("wqn", s), "wk", ("fold low", s - 1) if s else None)
        f = f_ps[:, :].rearrange("p (h c d) -> p h c d", h=FH, c=2)
        def issue(e):
            for h in range(FH):
                for c in range(2):
                    ins = e.matmul(f[:, h, c, :], wqn_sb[:, r, h, c * P:(c + 1) * P],
                                   wk_sb[:, s * FH + h, :], start=True, stop=True)
            return ins
        pe.go(issue, done=("fold", s))
        act.need(("fold", s), free)
        act.go(lambda e: e.activation(weff[:, r, :, 0::2, 0:KVL], f, ACT.Copy),
               done=("fold high", s))
        dve.need(("fold high", s))
        dve.go(lambda e: e.tensor_tensor(
            weff[:, r, :, 1::2, 0:KVL], f, f32(weff[:, r, :, 0::2, 0:KVL]), ALU.subtract),
            done=("fold low", s))
        rot = wqp_sb[:, r, :, :].rearrange("p c (h d) -> p h c d", h=FH)
        pool.need(("wqp", s), free)
        pool.go(lambda e: e.tensor_copy(weff[:, r, :, 0::2, KVL:P], rot), done=("rot high", s))
        pool.need(("rot high", s))
        pool.go(lambda e: e.tensor_tensor(
            weff[:, r, :, 1::2, KVL:P], rot, f32(weff[:, r, :, 0::2, KVL:P]), ALU.subtract),
            done=("rot", s))
        sync.need(("fold low", s), ("rot", s))
        sync.load(lambda e: e.dma_start(
            f32(weff_dram[heads]).rearrange("h p n -> p h n"),
            f32(weff[:, r, :, :, :]).rearrange("p h c n -> p h (c n)")),
            ("weff out", s), core.dma_sem(f"weffo{r}"))

    return load, fold


def prologue(core, ctx, sb, pb, ident, x_t, wa, qw, kvw, rope_k, q_lat, k_high, k_low, lat2,
             wqn, wqp, wk, weff_dram):
    stages = latents(core, ctx, sb, pb, ident, x_t, wa, qw, kvw, rope_k, q_lat, k_high, k_low,
                     lat2)
    load, fold = fold_queries(core, ctx, sb, pb, wqn, wqp, wk, weff_dram)
    steps = NH // FH
    for step in range(max(NT + len(stages) - 1, 2 * steps + 4)):
        for n, stage in enumerate(stages):
            if 0 <= step - n < NT:
                stage(step - n)
        if step % 2 == 0 and 0 <= step // 2 - 2 < steps:
            fold(step // 2 - 2)
        if step % 2 == 0 and step // 2 < steps:
            load(step // 2)
    for s in (steps - 2, steps - 1):
        core.sync.need(("weff out", s))


def attention(core, ctx, sb, pb, ident, rope_q, far, q_lat, k_high, k_low, lat2, weff_dram,
              m_dram, wv, wo, attn_dram):
    pe, act, dve, pool, sync = core.pe, core.act, core.dve, core.pool, core.sync
    CW = 512
    PAIR = 2 * P
    cos_q = sb(ctx, "cos_q", [P, SEQ])
    sin_q = sb(ctx, "sin_q", [P, SEQ])
    far_sb = sb(ctx, "far_sb", [P, SEQ])
    weff = sb(ctx, "weff_in", [P, 2, 4, P], F32R)
    m_in = sb(ctx, "m_in", [P, 2, GK, 2, DM], F32R)
    wv_sb = sb(ctx, "wv_sb", [P, 2, KVL])
    wo_sb = sb(ctx, "wo_sb", [P, 2, DM])
    q_raw = sb(ctx, "q_raw", [P, CW])
    qf = sb(ctx, "qf", [P, CW])
    qs = sb(ctx, "qs", [P, CW])
    q_high = sb(ctx, "q_high", [P, 2, SEQ], F32R)
    q_low = sb(ctx, "q_low", [P, 2, SEQ], F32R)
    nbias = sb(ctx, "nbias", [P, 4])
    rsum = sb(ctx, "rsum", [P, 4])
    rinv = sb(ctx, "rinv", [P, 4])
    NPR = 3
    prob = sb(ctx, "prob", [P, NPR, SEQ])
    pt_high = sb(ctx, "pt_high", [P, 2, JT, PAIR], F32R)
    pt_low = sb(ctx, "pt_low", [P, 2, JT, PAIR], F32R)
    o_part = sb(ctx, "o_part", [P, CW])
    o_sum = sb(ctx, "o_sum", [P, SEQ])
    ot_high = sb(ctx, "ot_high", [P, 2, GK, SEQ], F32R)
    ot_low = sb(ctx, "ot_low", [P, 2, GK, SEQ], F32R)
    acc = sb(ctx, "acc", [P, JT, DM])
    s_ps = [pb(ctx, f"s_ps{i}", 1024) for i in range(2)]
    p_ps = [pb(ctx, f"p_ps{i}") for i in range(2)]
    x_ps = pb(ctx, "x_ps")
    o_ps = pb(ctx, "o_ps")

    for name, dst, src in (("cos_q", cos_q[:, :], rope_q[0]),
                           ("sin_q", sin_q[KVL:P, :], rope_q[1][KVL:P, :]),
                           ("far", far_sb[:, :], far)):
        sync.load(lambda e, dst=dst, src=src: e.dma_start(dst, src), name, core.dma_sem(name))

    heads = [(b, h) for b in range(BATCH) for h in range(NH)]
    order = [2 * u + side for u in UNITS for side in range(2)]
    jobs = [(n, j) for n in range(len(heads)) for j in order]
    n_groups = len(heads) // GH
    x_read = [None]
    p_turn = [0]
    p_read = [None, None]

    def queries_load(n):
        if n >= 2:
            sync.need(("Q", n - 2, 1))
        sync.load(lambda e: e.dma_start(
            f32(weff[:, n % 2, :, :]).rearrange("p c n -> p (c n)"),
            f32(weff_dram[heads[n][1]])), ("weff", n), core.dma_sem(f"weff{n % 2}"))

    def queries(n, c):
        b, r = heads[n][0], n % 2
        tok = slice(b * SEQ + c * CW, b * SEQ + (c + 1) * CW)
        col = slice(c * CW, (c + 1) * CW)
        w = weff[:, r, :, :]
        pe.need(("weff", n), x_read[0])
        pairs = split_passes(w[:, 0, :], w[:, 1, :], q_lat["a_high"][:, tok],
                             q_lat["a_low"][:, tok])
        pairs += [(w[:, 2, :], q_lat["b_both"][:, tok]),
                  (w[0:QB, 3, :], q_lat["b_both"][0:QB, tok])]
        pe.go(lambda e: mm_chain(e, x_ps[:, :], pairs), done=("Q", n, c))
        before = ("q turned", n, 0) if c else ("q turned", n - 1, 1) if n else None
        act.need(("Q", n, c), before)
        act.go(lambda e: e.activation(q_raw[:, :], x_ps[:, :], ACT.Copy), done=("q raw", n, c))
        x_read[0] = ("q raw", n, c)

    def queries_turn(n, c):
        col = slice(c * CW, (c + 1) * CW)
        pool.need(("q raw", n, c), "cos_q", "sin_q", pool_last[0])
        pool.go(lambda e: e.tensor_tensor(qf[:, :], q_raw[:, :], cos_q[:, col], ALU.mult),
                done=("q cos", n, c))
        pool.need(("q cos", n, c))
        for to, at in ((KVL, KVL + HALF), (KVL + HALF, KVL)):
            pool.go(lambda e, to=to, at=at: e.tensor_tensor(
                qs[to:to + HALF, :], q_raw[at:at + HALF, :], sin_q[at:at + HALF, col],
                ALU.mult), done=("q sin", n, c, to))
            pool.need(("q sin", n, c, to))
        pool.go(lambda e: e.tensor_tensor(qf[KVL:P, :], qf[KVL:P, :], qs[KVL:P, :],
                                          ALU.add), done=("q turned", n, c))
        pool_last[0] = ("q turned", n, c)

    def queries_split(n, c):
        r = n % 2
        col = slice(c * CW, (c + 1) * CW)
        act.need(("q turned", n, c), ("S", n - 2, order[-1]) if n >= 2 else None)
        act.go(lambda e: e.activation(q_high[:, r, col], qf[:, :], ACT.Copy),
               done=("q high", n, c))
        pool.need(("q high", n, c), pool_last[0])
        pool.go(lambda e: e.tensor_tensor(q_low[:, r, col], qf[:, :],
                                          f32(q_high[:, r, col]), ALU.subtract),
                done=("q split", n, c))
        pool_last[0] = ("q split", n, c)

    pool_last = [None]

    def halves(j):
        width = (j + 1) * P
        return [(c, min(CW, width - c)) for c in range(0, width, CW)]

    def scores(i):
        n, j = jobs[i]
        b, r = heads[n][0], n % 2
        s = s_ps[i % 2]
        q = slice(j * P, (j + 1) * P)
        pe.need(("q split", n, j * P // CW), ("exp", i - 2) if i >= 2 else None)
        def issue(e):
            for c, w in halves(j):
                keys = slice(b * SEQ + c, b * SEQ + c + w)
                ins = mm_chain(e, s[:, c:c + w], split_passes(
                    q_high[:, r, q], q_low[:, r, q], k_high[:, keys], k_low[:, keys]))
            return ins
        pe.go(issue, done=("S", n, j))
        width = (j + 1) * P
        dve.need(("S", n, j), "far")
        dve.go(lambda e: e.tensor_tensor_reduce(
            out=s[:, 0:width], in0=s[:, 0:width], in1=far_sb[:, SEQ - width:SEQ], scale=1.0,
            scalar=3e38, op0=ALU.add, op1=ALU.min, accum_out=nbias[:, i % 4:i % 4 + 1]),
            done=("bias", i))

    def exponential(i):
        n, j = jobs[i]
        width = (j + 1) * P
        k = i % 4
        act.need(("bias", i), ("PT", i - NPR) if i >= NPR else None,
                 ("rinv", i - 4) if i >= 4 else None)
        act.go(lambda e: e.activation(prob[:, i % NPR, 0:width], s_ps[i % 2][:, 0:width],
                                      ACT.Exp, bias=nbias[:, k:k + 1], scale=-1.0,
                                      accum_out=rsum[:, k:k + 1]), done=("exp", i))

    def invert_sum(i):
        k = i % 4
        dve.need(("exp", i), ("norm", i - 4) if i >= 4 else None)
        dve.go(lambda e: e.reciprocal(rinv[:, k:k + 1], rsum[:, k:k + 1]), done=("rinv", i))

    def normalise(i):
        n, j = jobs[i]
        width = (j + 1) * P
        k = i % 4
        p = prob[:, i % NPR, 0:width]
        dve.need(("rinv", i))
        dve.go(lambda e: e.tensor_scalar(p, p, rinv[:, k:k + 1], None, ALU.mult),
               done=("norm", i))

    def transpose_probs(i):
        n, j = jobs[i]
        unit, side = i // 2, i % 2
        slot = unit % 2
        for c, w in halves(j):
            bank = p_turn[0] % 2
            p_turn[0] += 1
            pe.need(("norm", i), p_read[bank])
            def issue(e, c=c, w=w, bank=bank):
                for t in range(0, w, P):
                    ins = e.transpose(p_ps[bank][:, t:t + P],
                                      prob[:, i % NPR, c + t:c + t + P], ident[:, :])
                return ins
            last = c + w == (j + 1) * P
            name = ("PT", i) if last else ("PT", i, c)
            pe.go(issue, done=name)
            src = p_ps[bank][:, 0:w].rearrange("p (t s) -> p t s", s=P)
            to = (slice(None), slot, slice(c // P, (c + w) // P), slice(side * P, side * P + P))
            act.need(name, ("PV", unit - 2) if unit >= 2 else None)
            act.go(lambda e, src=src, to=to: e.activation(pt_high[to], src, ACT.Copy),
                   done=("pt high", i, c))
            dve.need(("pt high", i, c))
            dve.go(lambda e, src=src, to=to: e.tensor_tensor(
                pt_low[to], src, f32(pt_high[to]), ALU.subtract), done=("pt low", i, c))
            p_read[bank] = ("pt low", i, c)

    def values(unit, part):
        n, j = jobs[2 * unit]
        b = heads[n][0]
        slot, at = unit % 2, unit % 2 * PAIR
        pe.need(*[("pt low", i, c) for i in (2 * unit, 2 * unit + 1)
                  for c, _ in halves(jobs[i][1])])
        if unit >= 2 and unit % 2 == 0:
            pe.need(("O", unit // 2 - 1))
        work = [(0, 0, pt_high)]
        work += [(j + 1, P, probs) for probs in (pt_high, pt_low)]
        work += [(t, 0, probs) for t in range(1, j + 1) for probs in (pt_high, pt_low)]
        work += [(0, 0, pt_low)]
        cut = len(work) // 2
        mine = range(cut) if part == 0 else range(cut, len(work))
        def issue(e):
            for m in mine:
                t, c, probs = work[m]
                ins = e.matmul(o_ps[:, at + c:at + PAIR], lat2[:, b * JT + t, :],
                               probs[:, slot, t, c:PAIR], start=m == 0,
                               stop=m == len(work) - 1)
            return ins
        pe.go(issue, done=("PV", unit) if part else None)

    def half_head(t, c):
        first, second = UNITS[2 * c:2 * c + 2]
        return t.rearrange("p (u w) -> p u w", w=PAIR)[:, first:second + 1:second - first, :]

    def collect(k):
        n, c = k // 2, k % 2
        mine = slice(0, KVL) if n % 2 == 0 else slice(KVL, P)
        other = slice(KVL, P) if n % 2 == 0 else slice(0, KVL)
        act.need(("PV", 2 * k + 1), ("O", k - 1) if k else None)
        act.go(lambda e: e.activation(o_part[mine, :], o_ps[other, :], ACT.Copy),
               done=("o part", k))
        dve.need(("o part", k), ("ot low", n - 2 + (n + 1) % 2, c) if n >= 2 else None)
        dve.go(lambda e: e.tensor_tensor(
            half_head(o_sum[mine, :], c), o_ps[mine, :].rearrange("p (u w) -> p u w", w=PAIR),
            o_part[mine, :].rearrange("p (u w) -> p u w", w=PAIR), ALU.add), done=("O", k))

    def collect_split(k):
        n, c = k // 2, k % 2
        if n % 2 == 0:
            return
        g, kt = n // GH, n % GH // 2
        summed = half_head(o_sum[:, :], c)
        high, low = (half_head(t[:, g % 2, kt, :], c) for t in (ot_high, ot_low))
        act.need(("O", k), ("OP", g - 2, JT - 1) if g >= 2 else None)
        act.go(lambda e: e.activation(high, summed, ACT.Copy),
               done=("ot high", n, c))
        pool.need(("ot high", n, c), pool_last[0])
        pool.go(lambda e: e.tensor_tensor(low, summed, f32(high), ALU.subtract),
                done=("ot low", n, c))
        pool_last[0] = ("ot low", n, c)

    def values_weights_load(p):
        if p >= 1:
            sync.need(("M", p - 1))
        sync.load(lambda e: e.dma_start(wv_sb[:, :, :], wv[:, 2 * p:2 * p + 2, :]),
                  ("wv", p), core.dma_sem("wv"))
        sync.load(lambda e: e.dma_start(wo_sb[:, :, :], wo[:, 2 * p:2 * p + 2, :]),
                  ("wo", p), core.dma_sem("wo"))

    def fold_values(p):
        g, kt = p // GK, p % GK
        pe.need(("wv", p), ("wo", p), x_read[0])
        def issue(e):
            for n in range(2):
                ins = e.matmul(x_ps[n * KVL:(n + 1) * KVL, :], wv_sb[:, n, :], wo_sb[:, n, :],
                               start=True, stop=True)
            return ins
        pe.go(issue, done=("M", p))
        act.need(("M", p), ("OP", g - 2, JT - 1) if g >= 2 else None,
                 ("m out", g - 2) if g >= 2 else None)
        act.go(lambda e: e.activation(m_in[:, g % 2, kt, 0, :], x_ps[:, :], ACT.Copy),
               done=("m high", p))
        dve.need(("m high", p))
        dve.go(lambda e: e.tensor_tensor(m_in[:, g % 2, kt, 1, :], x_ps[:, :],
                                         f32(m_in[:, g % 2, kt, 0, :]), ALU.subtract),
               done=("m low", p))
        x_read[0] = ("m low", p)
        if kt == GK - 1:
            core.reached["m", g] = core.reached["m low", p]
            sync.need(("m low", p))
            sync.load(lambda e: e.dma_start(
                f32(m_dram[g]), f32(m_in[:, g % 2, :, :, :]).rearrange("p k c n -> p (k c n)")),
                ("m out", g), core.dma_sem(f"m_out{g % 2}"))

    def output_load(g):
        sync.need(("OP", g - 2, JT - 1), ("m out", g - 2) if g < NG + 2 else None,
                  ("m out", g % NG))
        sync.load(lambda e: e.dma_start(
            f32(m_in[:, g % 2, :, :, :]).rearrange("p k c n -> p (k c n)"),
            f32(m_dram[g % NG])), ("m", g), core.dma_sem(f"m_in{g % 2}"))

    tail_turn = [0]
    x_bank = x_ps[:, :]
    s_read = [("exp", len(jobs) - 1)] * 2

    def output_project(g, j, tail):
        tile = slice(j * P, (j + 1) * P)
        r, last = g % 2, g * GH + GH - 1
        bank, free = x_bank, x_read[0]
        if tail:
            turn = tail_turn[0] % 3
            tail_turn[0] += 1
            if turn:
                bank, free = s_ps[turn - 1][:, 0:CW], s_read[turn - 1]
                s_read[turn - 1] = ("sum", g, j)
        pe.need(("ot low", last, UNITS.index(j // 2) // 2), ("m", g), free)
        pairs = []
        for k in range(GK):
            pairs += split_passes(ot_high[:, r, k, tile], ot_low[:, r, k, tile],
                                  m_in[:, r, k, 0, :], m_in[:, r, k, 1, :])
        pe.go(lambda e: mm_chain(e, bank, pairs), done=("OP", g, j))
        if g % NG == 0:
            act.need(("OP", g, j), ("attn out", g // NG - 1, j) if g else None)
            act.go(lambda e: e.activation(acc[:, j, :], bank, ACT.Copy),
                   done=("sum", g, j))
        else:
            dve.need(("OP", g, j), ("sum", g - 1, j))
            dve.go(lambda e: e.tensor_tensor(acc[:, j, :], bank, acc[:, j, :],
                                             ALU.add), done=("sum", g, j))
        if bank is x_bank:
            x_read[0] = ("sum", g, j)
        if g % NG == NG - 1:
            b = g // NG
            sync.need(("sum", g, j))
            sync.load(lambda e: e.dma_start(attn_dram[b * JT + j], acc[:, j, :]),
                      ("attn out", b, j), core.dma_sem(f"attn{j}"))

    queries_load(0)
    queries_load(1)
    values_weights_load(0)
    for c in range(2):
        queries(0, c)
        queries_turn(0, c)
        queries_split(0, c)
    group_jobs = GH * JT
    spread = {JT * (j // 2 + 1) + O_STEPS[j % 2]: j for j in range(JT)}
    end = {LAG + 4 + j: j for j in range(JT)}
    for i in range(len(jobs) + max(end) + 1):
        n, j = jobs[i] if i < len(jobs) else (None, None)
        before = 0 <= i - 1 < len(jobs)
        done = i - LAG - 1
        if n is not None:
            scores(i)
        if before:
            invert_sum(i - 1)
        if 0 <= i - LAG < len(jobs):
            transpose_probs(i - LAG)
        if 1 <= done <= len(jobs):
            values((done - 1) // 2, (done - 1) % 2)
            if done % 4 == 0:
                collect(done // 4 - 1)
        if before:
            normalise(i - 1)
        if n is not None:
            exponential(i)
        if 5 <= done <= len(jobs) + 1 and done % 4 == 1:
            collect_split(done // 4 - 1)
        for c in range(2):
            at = i - Q_STEPS[c]
            m = at // JT + 1
            if at >= 0 and at % JT == 0 and m < len(heads):
                queries(m, c)
                queries_turn(m, c)
                if c == 1 and m + 1 < len(heads):
                    queries_load(m + 1)
            at -= Q_SPLIT
            m = at // JT + 1
            if at >= 0 and at % JT == 0 and m < len(heads):
                queries_split(m, c)
        for g in (i // group_jobs - 1, i // group_jobs - 2):
            k = i - (g + 1) * group_jobs
            output_at = end if g == n_groups - 1 else spread
            if 0 <= g < n_groups and k in output_at:
                output_project(g, output_at[k], tail=g == n_groups - 1)
                if output_at[k] == JT - 1 and NG <= g + 2 < n_groups:
                    output_load(g + 2)
        if n is not None:
            b, h = heads[n]
            if b == 0 and i % JT == M_STEP and h % GH >= GH - GK:
                p = h // GH * GK + h % GH - (GH - GK)
                fold_values(p)
                if p + 1 < NH // 2:
                    values_weights_load(p + 1)
    for j in range(JT):
        for b in range(BATCH):
            sync.need(("attn out", b, j))


def feed_forward(core, ctx, sb, pb, ident, x_t, x2_dram, attn_dram, wg, wu, wd, sg, su, sd,
                 out_t):
    pe, act, dve, pool, sync = core.pe, core.act, core.dve, core.pool, core.sync
    TT = TB // P
    xt_high = sb(ctx, "ft_high", [P, KD, TOKENS], F32R)
    xt_low = sb(ctx, "ft_low", [P, KD, TOKENS], F32R)
    raw = sb(ctx, "w_raw", [P, 3, KD * FG * P], I32)
    w_high = sb(ctx, "w_high", [P, 2, 3, KD * FG * P], F32R)
    w_low = sb(ctx, "w_low", [P, 2, 3, KD * FG * P], F32R)
    scale = sb(ctx, "scale", [P, 3])
    acc = sb(ctx, "f_acc", [P, NT, DM])
    xin = sb(ctx, "f_xin", [P, TT, DM])
    tmp = sb(ctx, "f_tmp", [P, 2, DM])
    stats = sb(ctx, "f_stats", [P, 3, NT, 6])
    mv = sb(ctx, "f_mv", [P, 3, NT, 2])
    dev = sb(ctx, "f_dev", [P, 3, NT])
    rstd = sb(ctx, "f_rstd", [P, 3, NT])
    gate = sb(ctx, "gate", [P, 2, TB])
    mid = sb(ctx, "mid", [P, 2, TB])
    mid_high = sb(ctx, "mid_high", [P, 2, FG, TB], F32R)
    mid_low = sb(ctx, "mid_low", [P, 2, FG, TB], F32R)
    eps = sb(ctx, "eps2", [P, 1])
    t_ps = [pb(ctx, f"ft_ps{i}") for i in range(2)]
    g_ps = [pb(ctx, f"fg_ps{i}") for i in range(2)]
    u_ps = [pb(ctx, f"fu_ps{i}") for i in range(2)]
    d_ps = [pb(ctx, f"fd_ps{i}") for i in range(2)]
    dve.go(lambda e: e.memset(eps[:, :], LN_EPS), done="eps2")

    def hidden(g):
        return g * FG * P, min(FG * P, HID - g * FG * P)

    def weight_views(t, g, n):
        h0, hw = hidden(g)
        if n < 2:
            return t[:, 0:KD * hw].rearrange("p (k h) -> p k h", k=KD)
        return t[:, 0:FG * DM].rearrange("p (k m) -> p k m", k=FG)

    def weight_parts(g, n):
        h0, hw = hidden(g)
        if n < 2:
            return [(P, slice(0, KD * hw))]
        return [(min(P, hw - k * P), slice(k * DM, (k + 1) * DM)) for k in range(-(-hw // P))]

    def weights_load(g):
        h0, hw = hidden(g)
        for n, w in enumerate((wg, wu, wd)):
            if g >= 1:
                sync.need(("w low", g - 1, n))
            dst = weight_views(raw[:, n, :], g, n)
            if n < 2:
                src = w[:, h0:h0 + hw].rearrange("(k p) h -> p k h", p=P)
                sync.load(lambda e, dst=dst, src=src: e.dma_start(dst, src), ("w", g, n, 0),
                          core.dma_sem(f"w_raw{n}"))
            else:
                for k, (rows, _) in enumerate(weight_parts(g, n)):
                    src = w[h0 + k * P:h0 + k * P + rows, :]
                    sync.load(lambda e, dst=dst, src=src, k=k, rows=rows: e.dma_start(
                        dst[0:rows, k, :], src), ("w", g, n, k), core.dma_sem(f"w_raw{n}{k}"))

    def weights_split(g, n):
        r = g % 2
        parts = weight_parts(g, n)
        for k, (rows, s) in enumerate(parts):
            act.need(("w", g, n, k), ("scale", n), ("D", g - 2, NTB - 1) if g >= 2 else None)
            act.go(lambda e, rows=rows, s=s: e.activation(
                w_high[0:rows, r, n, s], raw[0:rows, n, s], ACT.Copy,
                scale=scale[0:rows, n:n + 1]), done=("w high", g, n, k))
            dve.need(("w high", g, n, k))
            dve.go(lambda e, rows=rows, s=s: e.scalar_tensor_tensor(
                out=w_low[0:rows, r, n, s], in0=raw[0:rows, n, s],
                scalar=scale[0:rows, n:n + 1], in1=f32(w_high[0:rows, r, n, s]),
                op0=ALU.mult, op1=ALU.subtract),
                done=("w low", g, n) if k == len(parts) - 1 else None)

    def statistics(which, tiles, ready):
        for i in tiles:
            dve.need(ready(i))
            dve.go(lambda e, i=i: e.bn_stats(stats[:, which, i, :], acc[:, i, :]),
                   done=("fst", which, i))
        for i in tiles:
            dve.need(("fst", which, i))
            dve.go(lambda e, i=i: e.bn_aggr(mv[:, which, i, :], stats[:, which, i, :]),
                   done=("fmv", which, i))
        t = slice(tiles[0], tiles[-1] + 1)
        act.need(("fmv", which, tiles[-1]), "eps2")
        act.go(lambda e: e.activation(dev[:, which, t], mv[:, which, t, 1], ACT.Sqrt,
                                      bias=eps[:, :]), done=("fdev", which, tiles[0]))

    def inverse(which, tiles):
        t = slice(tiles[0], tiles[-1] + 1)
        dve.need(("fdev", which, tiles[0]))
        dve.go(lambda e: e.reciprocal(rstd[:, which, t], dev[:, which, t]),
               done=("frstd", which, tiles[0]))
        dve.need(("frstd", which, tiles[0]))

    def apply_norm(which, i, dst, done):
        dve.go(lambda e: e.tensor_scalar(dst, acc[:, i, :], mv[:, which, i, 0:1],
                                         rstd[:, which, i:i + 1], ALU.subtract, ALU.mult),
               done=done)

    def block(tb):
        return range(tb * TT, (tb + 1) * TT)

    def prepare_load(tb):
        for i in block(tb):
            sync.load(lambda e, i=i: e.dma_start(acc[:, i, :], attn_dram[i]), ("fa", i),
                      core.dma_sem(f"fa{i % TT}"))
            sync.need(("x2", i - TT) if i >= TT else None)
            sync.load(lambda e, i=i: e.dma_start(xin[:, i % TT, :], x_t[i]), ("fx", i),
                      core.dma_sem(f"fx{i % TT}"))

    def prepare_residual(tb):
        inverse(0, block(tb))
        for i in block(tb):
            apply_norm(0, i, acc[:, i, :], ("n0", i))
        for i in block(tb):
            dve.need(("n0", i), ("fx", i))
            dve.go(lambda e, i=i: e.tensor_tensor(acc[:, i, :], acc[:, i, :],
                                                  xin[:, i % TT, :], ALU.add),
                   done=("x2", i))
            sync.need(("x2", i))
            sync.load(lambda e, i=i: e.dma_start(x2_dram[i], acc[:, i, :]), ("x2 out", i),
                      core.dma_sem(f"x2o{i % TT}"))
        statistics(1, block(tb), lambda i: ("x2", i))

    def prepare_transpose(tb):
        inverse(1, block(tb))
        for i in block(tb):
            r = i % 2
            dve.need(("FT", i - 2) if i >= 2 else None)
            apply_norm(1, i, tmp[:, r, :], ("xf", i))
            pe.need(("xf", i), ("ft low", i - 2) if i >= 2 else None)
            def issue(e, i=i, r=r):
                for k in range(KD):
                    ins = e.transpose(t_ps[r][:, k * P:(k + 1) * P],
                                      tmp[:, r, k * P:(k + 1) * P], ident[:, :])
                return ins
            pe.go(issue, done=("FT", i))
            tok = slice(i * P, (i + 1) * P)
            view = t_ps[r][:, :].rearrange("p (k t) -> p k t", k=KD)
            act.need(("FT", i))
            act.go(lambda e, tok=tok, view=view: e.activation(xt_high[:, :, tok], view,
                                                              ACT.Copy), done=("ft high", i))
            dve.need(("ft high", i))
            dve.go(lambda e, tok=tok, view=view: e.tensor_tensor(
                xt_low[:, :, tok], view, f32(xt_high[:, :, tok]), ALU.subtract),
                done=("ft low", i))

    unit = [0]
    unit_of = {}

    def gate_up(g, tb, k):
        h0, hw = hidden(g)
        r, m = g % 2, blocks.index((g, tb)) % 2
        tok = slice(tb * TB, (tb + 1) * TB)
        rows = min(P, hw - k * P)
        n = unit[0]
        unit[0] += 1
        b = n % 2
        pe.need(("ft low", (tb + 1) * TT - 1), ("w low", g, 0), ("w low", g, 1),
                ("mid", n - 2) if n >= 2 else None)
        for which, bank in ((0, g_ps[b]), (1, u_ps[b])):
            wh = weight_views(w_high[:, r, which, :], g, which)
            wl = weight_views(w_low[:, r, which, :], g, which)
            cols = slice(k * P, k * P + rows)
            pairs = []
            for d in range(KD):
                pairs += split_passes(wh[:, d, cols], wl[:, d, cols], xt_high[:, d, tok],
                                      xt_low[:, d, tok])
            pe.go(lambda e, bank=bank, pairs=pairs: mm_chain(e, bank[0:rows, :], pairs),
                  done=("gu", n, which))
        act.need(("gu", n, 0), ("mid", n - 2) if n >= 2 else None)
        act.go(lambda e: e.activation(gate[0:rows, b, :], g_ps[b][0:rows, :], ACT.Silu),
               done=("silu", n))
        dve.need(("silu", n), ("gu", n, 1), ("mid low", n - 2) if n >= 2 else None)
        dve.go(lambda e: e.tensor_tensor(mid[0:rows, b, :], u_ps[b][0:rows, :],
                                         gate[0:rows, b, :], ALU.mult), done=("mid", n))
        at = blocks.index((g, tb))
        act.need(("mid", n), ("D", *blocks[at - 2]) if at >= 2 else None)
        act.go(lambda e: e.activation(mid_high[0:rows, m, k, :], mid[0:rows, b, :],
                                      ACT.Copy), done=("mid high", n))
        pool.need(("mid high", n))
        pool.go(lambda e: e.tensor_tensor(mid_low[0:rows, m, k, :], mid[0:rows, b, :],
                                          f32(mid_high[0:rows, m, k, :]), ALU.subtract),
                done=("mid low", n))
        unit_of[g, tb] = n

    down_turn = [0]
    d_read = [None, None]

    def down(g, tb, t):
        h0, hw = hidden(g)
        r, m = g % 2, blocks.index((g, tb)) % 2
        wh = weight_views(w_high[:, r, 2, :], g, 2)
        wl = weight_views(w_low[:, r, 2, :], g, 2)
        i = tb * TT + t
        b = down_turn[0] % 2
        down_turn[0] += 1
        pe.need(("mid low", unit_of[g, tb]), ("w low", g, 2), d_read[b])
        pairs = []
        for k in range(-(-hw // P)):
            rows = min(P, hw - k * P)
            s = slice(t * P, (t + 1) * P)
            pairs += split_passes(mid_high[0:rows, m, k, s], mid_low[0:rows, m, k, s],
                                  wh[0:rows, k, :], wl[0:rows, k, :])
        name = ("D", g, tb) if t == TT - 1 else ("D", g, tb, t)
        pe.go(lambda e: mm_chain(e, d_ps[b][:, :], pairs), done=name)
        if g == 0:
            act.need(name, ("x2 out", i), ("xf", i))
            act.go(lambda e: e.activation(acc[:, i, :], d_ps[b][:, :], ACT.Copy),
                   done=("part", g, i))
        else:
            dve.need(name, ("part", g - 1, i))
            dve.go(lambda e: e.tensor_tensor(acc[:, i, :], d_ps[b][:, :], acc[:, i, :],
                                             ALU.add), done=("part", g, i))
        d_read[b] = ("part", g, i)

    def finish_load(tb):
        for i in block(tb):
            sync.need(("y", i - TT) if i >= TT else ("x2", NT - TT + i))
            sync.load(lambda e, i=i: e.dma_start(xin[:, i % TT, :], x2_dram[i]), ("fx2", i),
                      core.dma_sem(f"fx{i % TT}"))

    def finish(tiles):
        inverse(2, tiles)
        for i in tiles:
            apply_norm(2, i, acc[:, i, :], ("n2", i))
        for i in tiles:
            dve.need(("n2", i), ("fx2", i))
            dve.go(lambda e, i=i: e.tensor_tensor(acc[:, i, :], acc[:, i, :],
                                                  xin[:, i % TT, :], ALU.add),
                   done=("y", i))
            sync.need(("y", i))
            sync.load(lambda e, i=i: e.dma_start(out_t[i], acc[:, i, :]), ("out", i),
                      core.dma_sem(f"out{i}"))

    blocks = [(g, tb) for pair in range(0, NFG, 2) for tb in range(NTB)
              for g in range(pair, min(pair + 2, NFG))]
    last = NFG - 1
    prepare_load(0)
    for n, s in enumerate((sg, su, sd)):
        sync.load(lambda e, n=n, s=s: e.dma_start(scale[:, n:n + 1], s.to_broadcast((P, 1))),
                  ("scale", n), core.dma_sem(f"scale{n}"))
    weights_load(0)
    statistics(0, block(0), lambda i: ("fa", i))
    prepare_residual(0)
    weights_split(0, 0)
    prepare_transpose(0)
    weights_split(0, 1)
    for n in range(len(blocks) + 1):
        g, tb = blocks[n] if n < len(blocks) else (None, None)
        if g is not None:
            ahead = g < 2 and tb + 1 < NTB
            if g == 0 and ahead:
                prepare_load(tb + 1)
            if (g, tb) == (0, 0):
                weights_split(0, 2)
                weights_load(1)
            if g == 0 and ahead and tb > 0:
                statistics(0, block(tb + 1), lambda i: ("fa", i))
            for k in range(-(-hidden(g)[1] // P)):
                gate_up(g, tb, k)
                if (g, tb) == (0, 0):
                    weights_split(1, k)
            if (g, tb) == (0, 0):
                weights_split(1, 2)
                weights_load(2)
                statistics(0, block(1), lambda i: ("fa", i))
            if g == 0 and ahead:
                prepare_residual(tb + 1)
            if g == 1 and ahead:
                prepare_transpose(tb + 1)
            if g == last and tb == 0:
                finish_load(0)
        if n >= 1:
            g0, tb0 = blocks[n - 1]
            for t in range(TT):
                down(g0, tb0, t)
                if g0 == last and tb0 == NTB - 1:
                    i = tb0 * TT + t
                    statistics(2, range(i, i + 1), lambda i: ("part", last, i))
                    if t >= 1:
                        finish(range(i - 1, i))
            if g0 == last and tb0 < NTB - 1:
                statistics(2, block(tb0), lambda i: ("part", last, i))
                finish(block(tb0))
                finish_load(tb0 + 1)
            if tb0 == NTB - 1 and g0 + 2 < NFG:
                for w in range(3):
                    weights_split(g0 + 2, w)
                if g0 + 3 < NFG:
                    weights_load(g0 + 3)
    finish(range(NT - 1, NT))
    for i in range(NT):
        sync.need(("out", i), ("x2 out", i))


def _tables():
    import numpy as np
    exponents = np.arange(0, ROPE, 2, dtype=np.float32) / np.float32(ROPE)
    freqs = np.float32(1.0) / np.power(np.float32(10000.0), exponents)
    angles = np.outer(np.arange(SEQ, dtype=np.float32), freqs.astype(np.float32))
    cos, sin = np.cos(angles), np.sin(angles)
    rope_k = np.concatenate([cos, cos, -sin, sin], axis=1).astype(np.float32)
    scale = -1.0 / np.sqrt(np.float64(NOPE + ROPE))
    rope_q = np.zeros((2, P, SEQ), np.float32)
    rope_q[0, 0:KVL] = scale
    rope_q[0, KVL:P] = np.concatenate([cos.T, cos.T]) * scale
    rope_q[1, KVL:P] = np.concatenate([sin.T, -sin.T]) * scale
    far = np.zeros((P, SEQ), np.float32)
    far[:, SEQ - P:] = np.where(np.arange(P)[None, :] > np.arange(P)[:, None], FAR, 0.0)
    return rope_k, rope_q, far


def kernel(**inputs):
    import numpy as np
    import concourse.bacc as bacc
    from concourse.bass_utils import run_bass_kernel_spmd

    get = lambda n: np.asarray(inputs[n])
    evens_odds = lambda a: np.concatenate([a[..., 0::2, :], a[..., 1::2, :]], axis=-2)
    wkv_a = get("L0_attn_wkv_a")
    wq_b = get("L0_attn_wq_b").reshape(NH, NOPE + ROPE, QL)
    wkv_b = get("L0_attn_wkv_b").reshape(NH, NOPE + VD, KVL)
    wa = np.concatenate([get("L0_attn_wq_a"), wkv_a[:KVL], evens_odds(wkv_a[KVL:])], axis=0).T
    twice = lambda a: np.concatenate([a, a[..., P:QL]], axis=-1)
    wqn = twice(wq_b[:, :NOPE]).transpose(1, 0, 2)
    wqp = twice(evens_odds(wq_b[:, NOPE:])).reshape(NH * ROPE, 2, P).transpose(2, 1, 0)
    rope_k, rope_q, far = _tables()
    arrays = {
        "x": get("L0_attn_x").reshape(TOKENS, DM),
        "wa": wa, "wqn": wqn, "wqp": wqp,
        "wk": wkv_b[:, :NOPE].transpose(1, 0, 2),
        "wv": wkv_b[:, NOPE:].transpose(1, 0, 2),
        "wo": get("L0_attn_wo").T.reshape(NH, VD, DM).transpose(1, 0, 2),
        "qw": twice(get("L0_attn_q_norm_w")).reshape(2, P).T,
        "kvw": get("L0_attn_kv_norm_w").reshape(1, KVL),
        "rope_k": rope_k, "rope_q": rope_q, "far": far,
        "wg": get("L0_ffn_w_gate").T, "wu": get("L0_ffn_w_up").T, "wd": get("L0_ffn_w_down").T,
        "sg": get("L0_ffn_scale_gate").reshape(1, 1),
        "su": get("L0_ffn_scale_up").reshape(1, 1),
        "sd": get("L0_ffn_scale_down").reshape(1, 1),
    }
    arrays = {n: np.ascontiguousarray(a) for n, a in arrays.items()}
    nc = bacc.Bacc("TRN2", target_bir_lowering=False, num_devices=1)
    args = [nc.dram_tensor(n, a.shape, mybir.dt.from_np(a.dtype), kind="ExternalInput").ap()
            for n, a in arrays.items()]
    out = nc.dram_tensor("out", (TOKENS, DM), F32, kind="ExternalOutput").ap()
    layer_kernel(nc, *args, out)
    result = run_bass_kernel_spmd(nc, [arrays], core_ids=[0])
    return result.results[0]["out"].reshape(BATCH, SEQ, DM)
```

```python
import concourse.bass as bass
from concourse import mybir
from contextlib import ExitStack

F32 = mybir.dt.float32
F32R = mybir.dt.float32r
I32 = mybir.dt.int32
ALU = mybir.AluOpType
ACT = mybir.ActivationFunctionType

P = 128
BATCH, SEQ, DM = 2, 1024, 512
TOKENS = BATCH * SEQ
NT = TOKENS // P
JT = SEQ // P
KD = DM // P
NH, NOPE, ROPE, VD = 32, 128, 64, 128
QL, KVL = 192, 64
HALF = ROPE // 2
QB = QL - P
AW = QL + KVL + ROPE
GH = 4
NG = NH // GH
GK = GH * KVL // P
HID = 1376
HT = -(-HID // P)
FG = 2
NFG = -(-HT // FG)
TB = 512
NTB = TOKENS // TB
FH = 4
LAG = 3
UNITS = (0, 1, 2, 3)
Q_STEPS, O_STEPS, M_STEP = (2, 6), (4, 7), 1
Q_SPLIT = 3
Q_DELAY, Q_SPLIT_EARLY = 1, 2
EARLY_START = -2
LN_EPS, RMS_EPS = 1e-5, 1e-6
FAR = 1e38


class Lane:

    def __init__(self, reached, sem=None):
        self.reached, self.sem, self.count, self.steps = reached, sem, 0, []
        self.passed = {}
        self.last = None

    def need(self, *names):
        for n in names:
            if n is not None:
                assert n in self.reached, n
                self.steps.append(("need", n))

    def go(self, issue, done=None):
        if done is not None:
            assert done not in self.reached, done
            self.count += 1
            self.reached[done] = (self.sem, self.count)
            self.last = done
        self.steps.append(("go", issue, self.sem if done is not None else None, 1))

    def load(self, issue, done, sem):
        assert done not in self.reached, done
        n = sem.count = sem.count + 16
        self.reached[done] = (sem, n)
        self.steps.append(("go", issue, sem, 16))

    def play(self, eng):
        for kind, what, *inc in self.steps:
            if kind == "need":
                sem, value = self.reached[what]
                if self.passed.get(sem.name, 0) < value:
                    self.passed[sem.name] = value
                    eng.wait_ge(sem.handle, value)
            else:
                ins = what(eng)
                if inc[0] is not None:
                    ins.then_inc(inc[0].handle, inc[1])
        self.steps = []


class Sem:
    def __init__(self, ctx, nc, name):
        self.name, self.count = name, 0
        self.handle = ctx.enter_context(nc.semaphore(name))


class Core:

    def __init__(self, ctx, nc):
        self.ctx, self.nc, self.reached, self.sems = ctx, nc, {}, {}
        self.pe, self.act, self.dve, self.pool = (
            Lane(self.reached, Sem(ctx, nc, f"s_{n}")) for n in ("pe", "act", "dve", "pool"))
        self.sync = Lane(self.reached)

    def dma_sem(self, name):
        if name not in self.sems:
            self.sems[name] = Sem(self.ctx, self.nc, f"s_{name}")
        return self.sems[name]

    def play(self):
        with self.nc.Block() as block:
            block.sync(self.sync.play)
            block.tensor(self.pe.play)
            block.vector(self.dve.play)
            block.scalar(self.act.play)
            block.gpsimd(self.pool.play)


def f32(ap):
    return ap.bitcast(F32)


def split_passes(a_high, a_low, b_high, b_low):
    return [(a_high, b_high), (a_high, b_low), (a_low, b_high)]


def mm_chain(eng, out, pairs):
    for n, (stationary, moving) in enumerate(pairs):
        ins = eng.matmul(out, stationary, moving, start=n == 0, stop=n == len(pairs) - 1)
    return ins


def layer_kernel(nc, x, wa, wqn, wqp, wk, wv, wo, qw, kvw, rope_k, rope_q, far, wg, wu, wd,
                 sg, su, sd, out):
    weff_dram = nc.dram_tensor("weff", (NH, P, 4 * P), F32R, kind="Internal").ap()
    m_dram = nc.dram_tensor("m_fold", (NG, P, GK * 2 * DM), F32R, kind="Internal").ap()
    attn_dram = nc.dram_tensor("attn_out", (NT, P, DM), F32, kind="Internal").ap()
    x2_dram = nc.dram_tensor("x_mid", (NT, P, DM), F32, kind="Internal").ap()
    x_t = x.rearrange("(n p) d -> n p d", p=P)
    out_t = out.rearrange("(n p) d -> n p d", p=P)

    with ExitStack() as whole:
        core = Core(whole, nc)

        def sb(ctx, name, shape, dt=F32):
            return ctx.enter_context(nc.sbuf_tensor(name, shape, dt))

        def pb(ctx, name, width=512):
            return ctx.enter_context(nc.psum_tensor(name, [P, width], F32))

        ident = sb(whole, "ident", [P, P])
        core.pool.go(lambda e: e.memset(ident[:, :], 0.0), done="ident zero")
        core.pool.need("ident zero")
        core.pool.go(lambda e: e.affine_select(
            out=ident[:, :], in_=ident[:, :], compare_op=ALU.not_equal, fill=1.0, base=0,
            pattern=[[-1, P]], channel_multiplier=1), done="ident")

        with ExitStack() as attn:
            q_lat = {
                "a_high": sb(attn, "qa_high", [P, TOKENS], F32R),
                "a_low": sb(attn, "qa_low", [P, TOKENS], F32R),
                "b_both": sb(attn, "qb_both", [P, TOKENS], F32R),
            }
            k_high = sb(attn, "k_high", [P, TOKENS], F32R)
            k_low = sb(attn, "k_low", [P, TOKENS], F32R)
            lat2 = sb(attn, "lat2", [P, NT, P], F32R)
            q_bufs = query_buffers(attn, sb)
            with ExitStack() as ctx:
                folding = {"bank": pb(ctx, "f_ps"), "read": None}
                start = prologue(core, ctx, sb, pb, ident, x_t, wa, qw, kvw, rope_k, q_lat,
                                 k_high, k_low, lat2, wqn, wqp, wk, weff_dram, folding)
                next(start)
            with ExitStack() as ctx:
                middle = attention(core, ctx, sb, pb, ident, rope_q, far, q_lat, k_high, k_low,
                                   lat2, q_bufs, weff_dram, m_dram, wv, wo, attn_dram, folding)
                next(middle)
        with ExitStack() as ctx:
            end = feed_forward(core, ctx, sb, pb, ident, x_t, x2_dram, attn_dram, wg, wu, wd,
                               sg, su, sd, out_t)
            next(end)
            for _ in start:
                next(middle)
            for _ in middle:
                next(end, None)
            for _ in end:
                pass
            core.play()


def query_buffers(ctx, sb):
    return {
        "cos": sb(ctx, "cos_q", [P, SEQ]),
        "sin": sb(ctx, "sin_q", [P, SEQ]),
        "weff": sb(ctx, "weff_in", [P, 2, 4, P], F32R),
        "wv": sb(ctx, "wv_sb", [P, 2, KVL]),
        "wo": sb(ctx, "wo_sb", [P, 2, DM]),
        "raw": sb(ctx, "q_raw", [P, 512]),
        "turned": sb(ctx, "qf", [P, 512]),
        "sines": sb(ctx, "qs", [P, 512]),
        "high": sb(ctx, "q_high", [P, 2, SEQ], F32R),
        "low": sb(ctx, "q_low", [P, 2, SEQ], F32R),
        "far": sb(ctx, "far_sb", [P, SEQ]),
    }


def latents(core, ctx, sb, pb, ident, x_t, wa, qw, kvw, rope_k, q_lat, k_high, k_low, lat2):
    pe, act, dve, pool, sync = core.pe, core.act, core.dve, core.pool, core.sync
    NX, NA = 4, 3
    wa_raw = sb(ctx, "wa_raw", [P, KD, AW])
    wa_high = sb(ctx, "wa_high", [P, KD, AW], F32R)
    wa_low = sb(ctx, "wa_low", [P, KD, AW], F32R)
    qw_col = sb(ctx, "qw_col", [P, 2])
    kvw_row = sb(ctx, "kvw_row", [P, KVL])
    rk = sb(ctx, "rope_k_sb", [P, JT, 4 * HALF])
    xin = sb(ctx, "xin", [P, NX, DM])
    stats = sb(ctx, "stats", [P, NT, 6])
    mv = sb(ctx, "mv", [P, NT, 2])
    dev = sb(ctx, "dev", [P, NT])
    rstd = sb(ctx, "rstd", [P, NT])
    xn = sb(ctx, "xn", [P, 2, DM])
    xt_high = sb(ctx, "xt_high", [P, 2, DM], F32R)
    xt_low = sb(ctx, "xt_low", [P, 2, DM], F32R)
    squares = sb(ctx, "squares", [P, 2, QL])
    ssum = sb(ctx, "ssum", [P, NT, 2])
    rms = sb(ctx, "rms", [P, NT, 2])
    rrms = sb(ctx, "rrms", [P, NT, 2])
    qn = sb(ctx, "qn", [P, 2, 2 * P])
    kk = sb(ctx, "kk", [P, 2, P])
    kv2 = sb(ctx, "kv2", [P, 2, ROPE])
    t_ps = [pb(ctx, f"t_ps{i}") for i in range(2)]
    a_ps = [pb(ctx, f"a_ps{i}") for i in range(NA)]
    u_ps = [pb(ctx, f"u_ps{i}") for i in range(2)]
    eps = sb(ctx, "eps1", [P, 2])
    dve.go(lambda e: e.memset(eps[:, 0:1], LN_EPS))
    dve.go(lambda e: e.memset(eps[:, 1:2], RMS_EPS), done="eps1")

    def load_x(i):
        if i >= NX:
            sync.need(("xn", i - NX))
        sync.load(lambda e: e.dma_start(xin[:, i % NX, :], x_t[i]), ("x", i),
                  core.dma_sem(f"x{i % NX}"))

    load_x(0)
    load_x(1)
    sync.load(lambda e: e.dma_start(wa_raw[:, :, :], wa.rearrange("(k p) n -> p k n", p=P)),
              "wa", core.dma_sem("wa"))
    load_x(2)
    for name, dst, src in (("qw", qw_col[:, :], qw),
                           ("kvw", kvw_row[:, :], kvw.to_broadcast((P, KVL))),
                           ("rk", rk[:, :, :], rope_k.rearrange("(j p) n -> p j n", p=P))):
        sync.load(lambda e, dst=dst, src=src: e.dma_start(dst, src), name, core.dma_sem(name))

    def split_wa():
        act.need("wa")
        act.go(lambda e: e.activation(wa_high[:, :, :], wa_raw[:, :, :], ACT.Copy), done="wa high")
        dve.need("wa high")
        dve.go(lambda e: e.tensor_tensor(wa_low[:, :, :], wa_raw[:, :, :], f32(wa_high[:, :, :]),
                                         ALU.subtract), done="wa low")

    def statistics(i):
        if i + 2 < NT and i >= 1:
            load_x(i + 2)
        dve.need(("x", i))
        dve.go(lambda e: e.bn_stats(stats[:, i, :], xin[:, i % NX, :]), done=("st", i))
        dve.need(("st", i))
        dve.go(lambda e: e.bn_aggr(mv[:, i, :], stats[:, i, :]), done=("mv", i))

    def deviation(i):
        act.need(("mv", i), "eps1")
        act.go(lambda e: e.activation(dev[:, i:i + 1], mv[:, i, 1:2], ACT.Sqrt,
                                      bias=eps[:, 0:1]), done=("dev", i))

    def normalise(i):
        dve.need(("dev", i))
        dve.go(lambda e: e.reciprocal(rstd[:, i:i + 1], dev[:, i:i + 1]), done=("rstd", i))
        dve.need(("rstd", i))
        if i >= 2:
            dve.need(("T", i - 2))
        dve.go(lambda e: e.tensor_scalar(xn[:, i % 2, :], xin[:, i % NX, :], mv[:, i, 0:1],
                                         rstd[:, i:i + 1], ALU.subtract, ALU.mult),
               done=("xn", i))

    def transpose_x(i):
        r = i % 2
        pe.need(("xn", i), "ident")
        if i >= 2:
            pe.need(("xt low", i - 2))
        def issue(e):
            for k in range(KD):
                ins = e.transpose(t_ps[r][:, k * P:(k + 1) * P], xn[:, r, k * P:(k + 1) * P],
                                  ident[:, :])
            return ins
        pe.go(issue, done=("T", i))
        act.need(("T", i))
        if i >= 2:
            act.need(("A", i - 2))
        act.go(lambda e: e.activation(xt_high[:, r, :], t_ps[r][:, :], ACT.Copy),
               done=("xt high", i))

    def transpose_x_low(i):
        r = i % 2
        dve.need(("xt high", i))
        dve.go(lambda e: e.tensor_tensor(xt_low[:, r, :], t_ps[r][:, :], f32(xt_high[:, r, :]),
                                         ALU.subtract), done=("xt low", i))

    def project(i):
        r = i % 2
        q = a_ps[i % NA]
        pe.need(("xt low", i), "wa low")
        if i >= NA:
            pe.need(("qn", i - NA))
        pairs = []
        for k in range(KD):
            s = slice(k * P, (k + 1) * P)
            pairs += split_passes(xt_high[:, r, s], xt_low[:, r, s], wa_high[:, k, :],
                                  wa_low[:, k, :])
        pe.go(lambda e: mm_chain(e, q[:, 0:AW], pairs), done=("A", i))
        act.need(("A", i), ("sk", i - 1) if i else None)
        act.go(lambda e: e.activation(squares[:, 0, :], q[:, 0:QL], ACT.Square,
                                      accum_out=ssum[:, i, 0:1]))
        act.go(lambda e: e.activation(squares[:, 1, 0:KVL], q[:, QL:QL + KVL], ACT.Square,
                                      accum_out=ssum[:, i, 1:2]), done=("sk", i))
        act.need(("sk", i))
        act.go(lambda e: e.activation(rms[:, i, 0:1], ssum[:, i, 0:1], ACT.Sqrt,
                                      bias=eps[:, 1:2], scale=1.0 / QL))
        act.go(lambda e: e.activation(rms[:, i, 1:2], ssum[:, i, 1:2], ACT.Sqrt,
                                      bias=eps[:, 1:2], scale=1.0 / KVL), done=("rms", i))

    def norm_keys(i):
        r, j = i % 2, i % JT
        q = a_ps[i % NA]
        pe_col = QL + KVL
        dve.need(("rms", i), "kvw", "rk")
        dve.go(lambda e: e.reciprocal(rrms[:, i, :], rms[:, i, :]), done=("rrms", i))
        dve.need(("rrms", i))
        if i >= 2:
            dve.need(("U", i - 2))
        dve.go(lambda e: e.scalar_tensor_tensor(
            out=kk[:, r, 0:KVL], in0=q[:, QL:pe_col], scalar=rrms[:, i, 1:2],
            in1=kvw_row[:, :], op0=ALU.mult, op1=ALU.mult))
        dve.go(lambda e: e.tensor_tensor(kk[:, r, KVL:P], q[:, pe_col:AW], rk[:, j, 0:ROPE],
                                         ALU.mult))
        dve.go(lambda e: e.tensor_tensor(kv2[:, r, 0:HALF], q[:, pe_col + HALF:AW],
                                         rk[:, j, ROPE:ROPE + HALF], ALU.mult))
        dve.go(lambda e: e.tensor_tensor(kv2[:, r, HALF:ROPE], q[:, pe_col:pe_col + HALF],
                                         rk[:, j, ROPE + HALF:2 * ROPE], ALU.mult),
               done=("kk2", i))
        pool.need(("kk2", i))
        pool.go(lambda e: e.tensor_tensor(kk[:, r, KVL:P], kk[:, r, KVL:P], kv2[:, r, :],
                                          ALU.add), done=("kk", i))
        pool.go(lambda e: e.tensor_copy(lat2[:, i, 0:KVL], kk[:, r, 0:KVL]), done=("lat high", i))
        pool.need(("lat high", i))
        pool.go(lambda e: e.tensor_tensor(lat2[:, i, KVL:P], kk[:, r, 0:KVL],
                                          f32(lat2[:, i, 0:KVL]), ALU.subtract),
                done=("lat", i))

    def norm_queries(i):
        r, q = i % 2, a_ps[i % NA]
        act.need(("kk2", i))
        act.go(lambda e: e.activation(qn[:, r, 0:QL], q[:, 0:QL], ACT.Copy,
                                      scale=rrms[:, i, 0:1]))
        act.go(lambda e: e.activation(qn[:, r, QL:2 * P], q[:, P:QL], ACT.Copy,
                                      scale=rrms[:, i, 0:1]), done=("qn", i))

    def transpose_latents(i):
        r = i % 2
        u = u_ps[r]
        tok = slice(i * P, (i + 1) * P)
        pe.need(("qn", i), ("lat", i))
        if i >= 2:
            pe.need(("k low", i - 2))
        def issue(e):
            e.transpose(u[:, 0:P], qn[:, r, 0:P], ident[:, :])
            e.transpose(u[:, P:2 * P], qn[:, r, P:2 * P], ident[:, :])
            return e.transpose(u[:, 2 * P:3 * P], kk[:, r, :], ident[:, :])
        pe.go(issue, done=("U", i))
        act.need(("U", i), "qw")
        act.go(lambda e: e.activation(q_lat["a_high"][:, tok], u[:, 0:P], ACT.Copy,
                                      scale=qw_col[:, 0:1]))
        act.go(lambda e: e.activation(q_lat["b_both"][:, tok], u[:, P:2 * P], ACT.Copy,
                                      scale=qw_col[:, 1:2]))
        act.go(lambda e: e.activation(k_high[:, tok], u[:, 2 * P:3 * P], ACT.Copy),
               done=("high", i))

    def transpose_latents_low(i):
        u = u_ps[i % 2]
        tok = slice(i * P, (i + 1) * P)
        dve.need(("high", i))
        dve.go(lambda e: e.scalar_tensor_tensor(
            out=q_lat["a_low"][:, tok], in0=u[:, 0:P], scalar=qw_col[:, 0:1],
            in1=f32(q_lat["a_high"][:, tok]), op0=ALU.mult, op1=ALU.subtract))
        low = q_lat["b_both"][QB:P, tok]
        dve.go(lambda e: e.scalar_tensor_tensor(
            out=low, in0=u[QB:P, P:2 * P], scalar=qw_col[QB:P, 1:2], in1=f32(low),
            op0=ALU.mult, op1=ALU.subtract))
        dve.go(lambda e: e.tensor_tensor(k_low[:, tok], u[:, 2 * P:3 * P], f32(k_high[:, tok]),
                                         ALU.subtract), done=("k low", i))

    split_wa()
    return [(4, norm_keys), (1, normalise), (0, statistics), (5, transpose_latents),
            (2, transpose_x), (5, transpose_latents_low), (2, transpose_x_low), (3, project),
            (4, norm_queries), (0, deviation)]


def fold_queries(core, ctx, sb, wqn, wqp, wk, weff_dram, folding):
    pe, act, dve, pool, sync = core.pe, core.act, core.dve, core.pool, core.sync
    wqn_sb = sb(ctx, "wqn_sb", [P, 2, FH, 2 * P])
    wqp_sb = sb(ctx, "wqp_sb", [P, 2, 2, FH * ROPE])
    wk_sb = sb(ctx, "wk_sb", [P, NH, KVL])
    weff = sb(ctx, "weff_sb", [P, 2, FH, 4, P], F32R)
    f_ps = folding["bank"]

    def load(s):
        r = s % 2
        heads = slice(s * FH, (s + 1) * FH)
        if s == 0:
            sync.load(lambda e: e.dma_start(wk_sb[:, :, :], wk), "wk", core.dma_sem("wk"))
        if s >= 2:
            sync.need(("fold", s - 2), ("rot", s - 2))
        sync.load(lambda e: e.dma_start(wqn_sb[:, r, :, :], wqn[:, heads, :]),
                  ("wqn", s), core.dma_sem(f"wqn{r}"))
        sync.load(lambda e: e.dma_start(
            wqp_sb[:, r, :, :], wqp[:, :, s * FH * ROPE:(s + 1) * FH * ROPE]),
            ("wqp", s), core.dma_sem(f"wqp{r}"))

    def fold(s):
        r = s % 2
        heads = slice(s * FH, (s + 1) * FH)
        free = ("weff out", s - 2) if s >= 2 else None
        pe.need(("wqn", s), "wk", folding["read"])
        f = f_ps[:, :].rearrange("p (h c d) -> p h c d", h=FH, c=2)
        def issue(e):
            for h in range(FH):
                for c in range(2):
                    ins = e.matmul(f[:, h, c, :], wqn_sb[:, r, h, c * P:(c + 1) * P],
                                   wk_sb[:, s * FH + h, :], start=True, stop=True)
            return ins
        pe.go(issue, done=("fold", s))
        act.need(("fold", s), free)
        act.go(lambda e: e.activation(weff[:, r, :, 0::2, 0:KVL], f, ACT.Copy),
               done=("fold high", s))
        dve.need(("fold high", s))
        dve.go(lambda e: e.tensor_tensor(
            weff[:, r, :, 1::2, 0:KVL], f, f32(weff[:, r, :, 0::2, 0:KVL]), ALU.subtract),
            done=("fold low", s))
        folding["read"] = ("fold low", s)
        rot = wqp_sb[:, r, :, :].rearrange("p c (h d) -> p h c d", h=FH)
        pool.need(("wqp", s), free)
        pool.go(lambda e: e.tensor_copy(weff[:, r, :, 0::2, KVL:P], rot), done=("rot high", s))
        pool.need(("rot high", s))
        pool.go(lambda e: e.tensor_tensor(
            weff[:, r, :, 1::2, KVL:P], rot, f32(weff[:, r, :, 0::2, KVL:P]), ALU.subtract),
            done=("rot", s))
        sync.need(("fold low", s), ("rot", s))
        sync.load(lambda e: e.dma_start(
            f32(weff_dram[heads]).rearrange("h p n -> p h n"),
            f32(weff[:, r, :, :, :]).rearrange("p h c n -> p h (c n)")),
            ("weff out", s), core.dma_sem(f"weffo{r}"))

    return load, fold


def prologue(core, ctx, sb, pb, ident, x_t, wa, qw, kvw, rope_k, q_lat, k_high, k_low, lat2,
             wqn, wqp, wk, weff_dram, folding):
    stages = latents(core, ctx, sb, pb, ident, x_t, wa, qw, kvw, rope_k, q_lat, k_high, k_low,
                     lat2)
    load, fold = fold_queries(core, ctx, sb, wqn, wqp, wk, weff_dram, folding)
    steps = NH // FH
    yield
    depth = max(n for n, _ in stages)
    ready = [half * SEQ // 2 // P + depth - 1 + Q_DELAY for half in (1, 2)]
    for step in range(max(NT + depth, 2 * steps + 4)):
        for n, stage in stages:
            if 0 <= step - n < NT:
                stage(step - n)
        if step % 2 == 0 and 0 <= step // 2 - 2 < steps:
            fold(step // 2 - 2)
        if step % 2 == 0 and step // 2 < steps:
            load(step // 2)
        if step == 6:
            yield
        for c in range(2):
            if step == ready[c] or step == ready[c] + Q_SPLIT_EARLY:
                yield


def attention(core, ctx, sb, pb, ident, rope_q, far, q_lat, k_high, k_low, lat2, q_bufs,
              weff_dram, m_dram, wv, wo, attn_dram, folding):
    pe, act, dve, pool, sync = core.pe, core.act, core.dve, core.pool, core.sync
    CW = 512
    PAIR = 2 * P
    cos_q, sin_q, weff, wv_sb, wo_sb, q_raw, qf, qs, q_high, q_low, far_sb = \
        q_bufs.values()
    m_in = sb(ctx, "m_in", [P, 2, GK, 2, DM], F32R)
    nbias = sb(ctx, "nbias", [P, 4])
    rsum = sb(ctx, "rsum", [P, 4])
    rinv = sb(ctx, "rinv", [P, 4])
    NPR = 3
    prob = sb(ctx, "prob", [P, NPR, SEQ])
    pt_high = sb(ctx, "pt_high", [P, 2, JT, PAIR], F32R)
    pt_low = sb(ctx, "pt_low", [P, 2, JT, PAIR], F32R)
    o_part = sb(ctx, "o_part", [P, CW])
    o_sum = sb(ctx, "o_sum", [P, SEQ])
    ot_high = sb(ctx, "ot_high", [P, 2, GK, SEQ], F32R)
    ot_low = sb(ctx, "ot_low", [P, 2, GK, SEQ], F32R)
    acc = sb(ctx, "acc", [P, JT, DM])
    s_ps = [pb(ctx, f"s_ps{i}", 1024) for i in range(2)]
    p_ps = [pb(ctx, f"p_ps{i}") for i in range(2)]
    x_ps = pb(ctx, "x_ps")
    o_ps = pb(ctx, "o_ps")

    yield

    def table_load(name, dst, src):
        sync.load(lambda e: e.dma_start(dst, src), name, core.dma_sem(name))

    heads = [(b, h) for b in range(BATCH) for h in range(NH)]
    order = [2 * u + side for u in UNITS for side in range(2)]
    jobs = [(n, j) for n in range(len(heads)) for j in order]
    n_groups = len(heads) // GH
    x_read = [None]
    p_turn = [0]
    p_read = [None, None]

    def queries_load(n):
        if n >= 2:
            sync.need(("Q", n - 2, 1))
        else:
            sync.need(("weff out", 0))
        sync.load(lambda e: e.dma_start(
            f32(weff[:, n % 2, :, :]).rearrange("p c n -> p (c n)"),
            f32(weff_dram[heads[n][1]])), ("weff", n), core.dma_sem(f"weff{n % 2}"))

    def queries(n, c):
        b, r = heads[n][0], n % 2
        tok = slice(b * SEQ + c * CW, b * SEQ + (c + 1) * CW)
        col = slice(c * CW, (c + 1) * CW)
        w = weff[:, r, :, :]
        bank = x_ps if n else folding["bank"]
        pe.need(("weff", n), x_read[0] if n else folding["read"])
        if n == 0:
            pe.need(("k low", (c + 1) * CW // P - 1))
        pairs = split_passes(w[:, 0, :], w[:, 1, :], q_lat["a_high"][:, tok],
                             q_lat["a_low"][:, tok])
        pairs += [(w[:, 2, :], q_lat["b_both"][:, tok]),
                  (w[0:QB, 3, :], q_lat["b_both"][0:QB, tok])]
        pe.go(lambda e: mm_chain(e, bank[:, :], pairs), done=("Q", n, c))
        before = ("q turned", n, 0) if c else ("q turned", n - 1, 1) if n else None
        act.need(("Q", n, c), before)
        act.go(lambda e: e.activation(q_raw[:, :], bank[:, :], ACT.Copy), done=("q raw", n, c))
        if n:
            x_read[0] = ("q raw", n, c)
        else:
            folding["read"] = ("q raw", n, c)

    def queries_turn(n, c):
        col = slice(c * CW, (c + 1) * CW)
        pool.need(("q raw", n, c), "cos_q", "sin_q", pool.last)
        pool.go(lambda e: e.tensor_tensor(qf[:, :], q_raw[:, :], cos_q[:, col], ALU.mult),
                done=("q cos", n, c))
        pool.need(("q cos", n, c))
        for to, at in ((KVL, KVL + HALF), (KVL + HALF, KVL)):
            pool.go(lambda e, to=to, at=at: e.tensor_tensor(
                qs[to:to + HALF, :], q_raw[at:at + HALF, :], sin_q[at:at + HALF, col],
                ALU.mult), done=("q sin", n, c, to))
            pool.need(("q sin", n, c, to))
        pool.go(lambda e: e.tensor_tensor(qf[KVL:P, :], qf[KVL:P, :], qs[KVL:P, :],
                                          ALU.add), done=("q turned", n, c))

    def queries_split(n, c):
        r = n % 2
        col = slice(c * CW, (c + 1) * CW)
        act.need(("q turned", n, c), ("S", n - 2, order[-1]) if n >= 2 else None)
        act.go(lambda e: e.activation(q_high[:, r, col], qf[:, :], ACT.Copy),
               done=("q high", n, c))
        pool.need(("q high", n, c), pool.last)
        pool.go(lambda e: e.tensor_tensor(q_low[:, r, col], qf[:, :],
                                          f32(q_high[:, r, col]), ALU.subtract),
                done=("q split", n, c))

    def halves(j):
        width = (j + 1) * P
        return [(c, min(CW, width - c)) for c in range(0, width, CW)]

    def scores(i):
        n, j = jobs[i]
        b, r = heads[n][0], n % 2
        s = s_ps[i % 2]
        q = slice(j * P, (j + 1) * P)
        pe.need(("q split", n, j * P // CW), ("exp", i - 2) if i >= 2 else None)
        def issue(e):
            for c, w in halves(j):
                keys = slice(b * SEQ + c, b * SEQ + c + w)
                ins = mm_chain(e, s[:, c:c + w], split_passes(
                    q_high[:, r, q], q_low[:, r, q], k_high[:, keys], k_low[:, keys]))
            return ins
        pe.go(issue, done=("S", n, j))
        width = (j + 1) * P
        dve.need(("S", n, j), "far")
        dve.go(lambda e: e.tensor_tensor_reduce(
            out=s[:, 0:width], in0=s[:, 0:width], in1=far_sb[:, SEQ - width:SEQ], scale=1.0,
            scalar=3e38, op0=ALU.add, op1=ALU.min, accum_out=nbias[:, i % 4:i % 4 + 1]),
            done=("bias", i))

    def exponential(i):
        n, j = jobs[i]
        width = (j + 1) * P
        k = i % 4
        act.need(("bias", i), ("PT", i - NPR) if i >= NPR else None,
                 ("rinv", i - 4) if i >= 4 else None)
        act.go(lambda e: e.activation(prob[:, i % NPR, 0:width], s_ps[i % 2][:, 0:width],
                                      ACT.Exp, bias=nbias[:, k:k + 1], scale=-1.0,
                                      accum_out=rsum[:, k:k + 1]), done=("exp", i))

    def invert_sum(i):
        k = i % 4
        dve.need(("exp", i), ("norm", i - 4) if i >= 4 else None)
        dve.go(lambda e: e.reciprocal(rinv[:, k:k + 1], rsum[:, k:k + 1]), done=("rinv", i))

    def normalise(i):
        n, j = jobs[i]
        width = (j + 1) * P
        k = i % 4
        p = prob[:, i % NPR, 0:width]
        dve.need(("rinv", i))
        dve.go(lambda e: e.tensor_scalar(p, p, rinv[:, k:k + 1], None, ALU.mult),
               done=("norm", i))

    def transpose_probs(i):
        n, j = jobs[i]
        unit, side = i // 2, i % 2
        slot = unit % 2
        for c, w in halves(j):
            bank = p_turn[0] % 2
            p_turn[0] += 1
            pe.need(("norm", i), p_read[bank])
            def issue(e, c=c, w=w, bank=bank):
                for t in range(0, w, P):
                    ins = e.transpose(p_ps[bank][:, t:t + P],
                                      prob[:, i % NPR, c + t:c + t + P], ident[:, :])
                return ins
            last = c + w == (j + 1) * P
            name = ("PT", i) if last else ("PT", i, c)
            pe.go(issue, done=name)
            src = p_ps[bank][:, 0:w].rearrange("p (t s) -> p t s", s=P)
            to = (slice(None), slot, slice(c // P, (c + w) // P), slice(side * P, side * P + P))
            act.need(name, ("PV", unit - 2) if unit >= 2 else None)
            act.go(lambda e, src=src, to=to: e.activation(pt_high[to], src, ACT.Copy),
                   done=("pt high", i, c))
            dve.need(("pt high", i, c))
            dve.go(lambda e, src=src, to=to: e.tensor_tensor(
                pt_low[to], src, f32(pt_high[to]), ALU.subtract), done=("pt low", i, c))
            p_read[bank] = ("pt low", i, c)

    def values(unit, part):
        n, j = jobs[2 * unit]
        b = heads[n][0]
        slot, at = unit % 2, unit % 2 * PAIR
        pe.need(*[("pt low", i, c) for i in (2 * unit, 2 * unit + 1)
                  for c, _ in halves(jobs[i][1])])
        if unit >= 2 and unit % 2 == 0:
            pe.need(("O", unit // 2 - 1))
        work = [(0, 0, pt_high)]
        work += [(j + 1, P, probs) for probs in (pt_high, pt_low)]
        work += [(t, 0, probs) for t in range(1, j + 1) for probs in (pt_high, pt_low)]
        work += [(0, 0, pt_low)]
        cut = len(work) // 2
        mine = range(cut) if part == 0 else range(cut, len(work))
        def issue(e):
            for m in mine:
                t, c, probs = work[m]
                ins = e.matmul(o_ps[:, at + c:at + PAIR], lat2[:, b * JT + t, :],
                               probs[:, slot, t, c:PAIR], start=m == 0,
                               stop=m == len(work) - 1)
            return ins
        pe.go(issue, done=("PV", unit) if part else None)

    def half_head(t, c):
        first, second = UNITS[2 * c:2 * c + 2]
        return t.rearrange("p (u w) -> p u w", w=PAIR)[:, first:second + 1:second - first, :]

    def collect(k):
        n, c = k // 2, k % 2
        mine = slice(0, KVL) if n % 2 == 0 else slice(KVL, P)
        other = slice(KVL, P) if n % 2 == 0 else slice(0, KVL)
        act.need(("PV", 2 * k + 1), ("summed", k - 1) if k else None,
                 ("ot low", n - 2 + (n + 1) % 2, c) if n >= 2 else None)
        act.go(lambda e: e.activation(
            half_head(o_sum[mine, :], c), o_ps[mine, :].rearrange("p (u w) -> p u w", w=PAIR),
            ACT.Copy))
        act.go(lambda e: e.activation(o_part[mine, :], o_ps[other, :], ACT.Copy),
               done=("O", k))
        pool.need(("O", k), pool.last)
        pool.go(lambda e: e.tensor_tensor(
            half_head(o_sum[mine, :], c), half_head(o_sum[mine, :], c),
            o_part[mine, :].rearrange("p (u w) -> p u w", w=PAIR), ALU.add),
            done=("summed", k))

    def collect_split(k):
        n, c = k // 2, k % 2
        if n % 2 == 0:
            return
        g, kt = n // GH, n % GH // 2
        summed = half_head(o_sum[:, :], c)
        high, low = (half_head(t[:, g % 2, kt, :], c) for t in (ot_high, ot_low))
        act.need(("summed", k), ("OP", g - 2, JT - 1) if g >= 2 else None)
        act.go(lambda e: e.activation(high, summed, ACT.Copy),
               done=("ot high", n, c))
        pool.need(("ot high", n, c), pool.last)
        pool.go(lambda e: e.tensor_tensor(low, summed, f32(high), ALU.subtract),
                done=("ot low", n, c))

    def values_weights_load(p):
        if p >= 1:
            sync.need(("M", p - 1))
        sync.load(lambda e: e.dma_start(wv_sb[:, :, :], wv[:, 2 * p:2 * p + 2, :]),
                  ("wv", p), core.dma_sem("wv"))
        sync.load(lambda e: e.dma_start(wo_sb[:, :, :], wo[:, 2 * p:2 * p + 2, :]),
                  ("wo", p), core.dma_sem("wo"))

    def fold_values(p):
        g, kt = p // GK, p % GK
        pe.need(("wv", p), ("wo", p), x_read[0])
        def issue(e):
            for n in range(2):
                ins = e.matmul(x_ps[n * KVL:(n + 1) * KVL, :], wv_sb[:, n, :], wo_sb[:, n, :],
                               start=True, stop=True)
            return ins
        pe.go(issue, done=("M", p))
        act.need(("M", p), ("OP", g - 2, JT - 1) if g >= 2 else None,
                 ("m out", g - 2) if g >= 2 else None)
        act.go(lambda e: e.activation(m_in[:, g % 2, kt, 0, :], x_ps[:, :], ACT.Copy),
               done=("m high", p))
        dve.need(("m high", p))
        dve.go(lambda e: e.tensor_tensor(m_in[:, g % 2, kt, 1, :], x_ps[:, :],
                                         f32(m_in[:, g % 2, kt, 0, :]), ALU.subtract),
               done=("m low", p))
        x_read[0] = ("m low", p)
        if kt == GK - 1:
            core.reached["m", g] = core.reached["m low", p]
            sync.need(("m low", p))
            sync.load(lambda e: e.dma_start(
                f32(m_dram[g]), f32(m_in[:, g % 2, :, :, :]).rearrange("p k c n -> p (k c n)")),
                ("m out", g), core.dma_sem(f"m_out{g % 2}"))

    def output_load(g):
        sync.need(("OP", g - 2, JT - 1), ("m out", g - 2) if g < NG + 2 else None,
                  ("m out", g % NG))
        sync.load(lambda e: e.dma_start(
            f32(m_in[:, g % 2, :, :, :]).rearrange("p k c n -> p (k c n)"),
            f32(m_dram[g % NG])), ("m", g), core.dma_sem(f"m_in{g % 2}"))

    tail_turn = [0]
    x_bank = x_ps[:, :]
    s_read = [("exp", len(jobs) - 1)] * 2

    def output_project(g, j, tail):
        tile = slice(j * P, (j + 1) * P)
        r, last = g % 2, g * GH + GH - 1
        bank, free = x_bank, x_read[0]
        if tail:
            turn = tail_turn[0] % 3
            tail_turn[0] += 1
            if turn:
                bank, free = s_ps[turn - 1][:, 0:CW], s_read[turn - 1]
                s_read[turn - 1] = ("sum", g, j)
        pe.need(("ot low", last, UNITS.index(j // 2) // 2), ("m", g), free)
        pairs = []
        for k in range(GK):
            pairs += split_passes(ot_high[:, r, k, tile], ot_low[:, r, k, tile],
                                  m_in[:, r, k, 0, :], m_in[:, r, k, 1, :])
        pe.go(lambda e: mm_chain(e, bank, pairs), done=("OP", g, j))
        if g % NG == 0:
            act.need(("OP", g, j), ("attn out", g // NG - 1, j) if g else None)
            act.go(lambda e: e.activation(acc[:, j, :], bank, ACT.Copy),
                   done=("sum", g, j))
        else:
            dve.need(("OP", g, j), ("sum", g - 1, j))
            dve.go(lambda e: e.tensor_tensor(acc[:, j, :], bank, acc[:, j, :],
                                             ALU.add), done=("sum", g, j))
        if bank is x_bank:
            x_read[0] = ("sum", g, j)
        if g % NG == NG - 1:
            b = g // NG
            sync.need(("sum", g, j))
            sync.load(lambda e: e.dma_start(attn_dram[b * JT + j], acc[:, j, :]),
                      ("attn out", b, j), core.dma_sem(f"attn{j}"))

    table_load("cos_q", cos_q[:, :], rope_q[0])
    table_load("sin_q", sin_q[KVL:P, :], rope_q[1][KVL:P, :])
    table_load("far", far_sb[:, :], far)
    values_weights_load(0)
    queries_load(0)
    yield
    queries(0, 0)
    queries_turn(0, 0)
    pool.need(pool.last)
    yield
    queries_split(0, 0)
    pool.need(pool.last)
    yield
    queries(0, 1)
    queries_turn(0, 1)
    pool.need(pool.last)
    yield
    queries_split(0, 1)
    pool.need(pool.last)
    yield
    queries_load(1)
    for lane in (pe, act, dve, pool, sync):
        lane.need(("U", NT - 1), ("high", NT - 1), ("k low", NT - 1), ("lat", NT - 1),
                  ("weff out", NH // FH - 2), ("weff out", NH // FH - 1))
    group_jobs = GH * JT
    spread = {JT * (j // 2 + 1) + O_STEPS[j % 2]: j for j in range(JT)}
    end = {LAG + 4 + j: j for j in range(JT)}
    for i in range(len(jobs) + max(end) + 1):
        n, j = jobs[i] if i < len(jobs) else (None, None)
        before = 0 <= i - 1 < len(jobs)
        done = i - LAG - 1
        if n is not None:
            scores(i)
        if before:
            invert_sum(i - 1)
        if 0 <= i - LAG < len(jobs):
            transpose_probs(i - LAG)
        if 1 <= done <= len(jobs):
            values((done - 1) // 2, (done - 1) % 2)
            if done % 4 == 0:
                collect(done // 4 - 1)
        if before:
            normalise(i - 1)
        if n is not None:
            exponential(i)
        if 5 <= done <= len(jobs) + 1 and done % 4 == 1:
            collect_split(done // 4 - 1)
        for c in range(2):
            at = i - Q_STEPS[c]
            m = at // JT + 1
            if at >= 0 and at % JT == 0 and m < len(heads):
                queries(m, c)
                queries_turn(m, c)
                if c == 1 and m + 1 < len(heads):
                    queries_load(m + 1)
            at -= Q_SPLIT
            m = at // JT + 1
            if at >= 0 and at % JT == 0 and m < len(heads):
                queries_split(m, c)
        for g in (i // group_jobs - 1, i // group_jobs - 2):
            k = i - (g + 1) * group_jobs
            output_at = end if g == n_groups - 1 else spread
            if 0 <= g < n_groups and k in output_at:
                output_project(g, output_at[k], tail=g == n_groups - 1)
                if output_at[k] == JT - 1 and NG <= g + 2 < n_groups:
                    output_load(g + 2)
        if i >= len(jobs) + EARLY_START:
            yield
        if n is not None:
            b, h = heads[n]
            if b == 0 and i % JT == M_STEP and h % GH >= GH - GK:
                p = h // GH * GK + h % GH - (GH - GK)
                fold_values(p)
                if p + 1 < NH // 2:
                    values_weights_load(p + 1)


def feed_forward(core, ctx, sb, pb, ident, x_t, x2_dram, attn_dram, wg, wu, wd, sg, su, sd,
                 out_t):
    pe, act, dve, pool, sync = core.pe, core.act, core.dve, core.pool, core.sync
    TT = TB // P
    last_head, last_group = BATCH * NH - 1, BATCH * NG - 1
    queries_over = ("q split", last_head, 1)
    latents_over = ("PV", BATCH * NH * JT // 2 - 1)
    attention_over = [("sum", last_group, j) for j in (JT - 1, JT - 2, JT - 3)]
    output_over = [("attn out", BATCH - 1, j) for j in range(JT)]
    xt_high, xt_low = [], []

    def transposed():
        n = len(xt_high)
        xt_high.append(sb(ctx, f"ft_high{n}", [P, KD, TB], F32R))
        xt_low.append(sb(ctx, f"ft_low{n}", [P, KD, TB], F32R))

    transposed()
    xins = [sb(ctx, "f_xin0", [P, TT, DM])]
    w_high = [sb(ctx, "w_high0", [P, 3, KD * FG * P], F32R)]
    w_low = [sb(ctx, "w_low0", [P, 3, KD * FG * P], F32R)]
    accs = [sb(ctx, "f_acc0", [P, TT, DM])]
    raw = sb(ctx, "w_raw", [P, 3, KD * FG * P], I32)
    scale = sb(ctx, "scale", [P, 3])
    stats = sb(ctx, "f_stats", [P, 3, NT, 6])
    mv = sb(ctx, "f_mv", [P, 3, NT, 2])
    dev = sb(ctx, "f_dev", [P, 3, NT])
    rstd = sb(ctx, "f_rstd", [P, 3, NT])
    eps = sb(ctx, "eps2", [P, 1])
    tmp = sb(ctx, "f_tmp", [P, 2, DM])
    gate = sb(ctx, "gate", [P, 2, TB])
    mid = sb(ctx, "mid", [P, 2, TB])
    mid_high = sb(ctx, "mid_high", [P, 2, FG, TB], F32R)
    mid_low = sb(ctx, "mid_low", [P, 2, FG, TB], F32R)
    w_high.append(sb(ctx, "w_high1", [P, 3, KD * FG * P], F32R))
    w_low.append(sb(ctx, "w_low1", [P, 3, KD * FG * P], F32R))
    for _ in range(1, NTB):
        transposed()
    accs += [sb(ctx, f"f_acc{n}", [P, TT, DM]) for n in range(1, NTB)]
    xins.append(sb(ctx, "f_xin1", [P, TT, DM]))
    early = [pb(ctx, f"f_ps{i}") for i in range(4)]
    t_ps = [pb(ctx, f"ft_ps{i}") for i in range(2)]
    d_ps = [pb(ctx, f"fd_ps{i}") for i in range(2)]
    g_ps, u_ps = early[1::-1], early[:1:-1]
    yield

    def acc(i):
        return accs[i // TT][:, i % TT, :]

    def xin(i):
        return xins[i // TT % 2][:, i % TT, :]

    for lane in (act, dve, pool, sync):
        lane.need(queries_over)
    dve.go(lambda e: e.memset(eps[:, :], LN_EPS), done="eps2")

    def hidden(g):
        return g * FG * P, min(FG * P, HID - g * FG * P)

    def weight_views(t, g, n):
        h0, hw = hidden(g)
        if n < 2:
            return t[:, 0:KD * hw].rearrange("p (k h) -> p k h", k=KD)
        return t[:, 0:FG * DM].rearrange("p (k m) -> p k m", k=FG)

    def weight_parts(g, n):
        h0, hw = hidden(g)
        if n < 2:
            return [(P, slice(0, KD * hw))]
        return [(min(P, hw - k * P), slice(k * DM, (k + 1) * DM)) for k in range(-(-hw // P))]

    def weights_load(g):
        h0, hw = hidden(g)
        for n, w in enumerate((wg, wu, wd)):
            if g >= 1:
                sync.need(("w low", g - 1, n))
            dst = weight_views(raw[:, n, :], g, n)
            if n < 2:
                src = w[:, h0:h0 + hw].rearrange("(k p) h -> p k h", p=P)
                sync.load(lambda e, dst=dst, src=src: e.dma_start(dst, src), ("w", g, n, 0),
                          core.dma_sem(f"w_raw{n}"))
            else:
                for k, (rows, _) in enumerate(weight_parts(g, n)):
                    src = w[h0 + k * P:h0 + k * P + rows, :]
                    sync.load(lambda e, dst=dst, src=src, k=k, rows=rows: e.dma_start(
                        dst[0:rows, k, :], src), ("w", g, n, k), core.dma_sem(f"w_raw{n}{k}"))

    def weights_split(g, n):
        r = g % 2
        parts = weight_parts(g, n)
        for k, (rows, s) in enumerate(parts):
            act.need(("w", g, n, k), ("scale", n),
                     ("D", g - 2, NTB - 1) if g >= 2 else latents_over)
            act.go(lambda e, rows=rows, s=s: e.activation(
                w_high[r][0:rows, n, s], raw[0:rows, n, s], ACT.Copy,
                scale=scale[0:rows, n:n + 1]), done=("w high", g, n, k))
            dve.need(("w high", g, n, k))
            dve.go(lambda e, rows=rows, s=s: e.scalar_tensor_tensor(
                out=w_low[r][0:rows, n, s], in0=raw[0:rows, n, s],
                scalar=scale[0:rows, n:n + 1], in1=f32(w_high[r][0:rows, n, s]),
                op0=ALU.mult, op1=ALU.subtract),
                done=("w low", g, n) if k == len(parts) - 1 else None)

    def moments(which, tiles, ready):
        for i in tiles:
            dve.need(ready(i))
            dve.go(lambda e, i=i: e.bn_stats(stats[:, which, i, :], acc(i)),
                   done=("fst", which, i))
        for i in tiles:
            dve.need(("fst", which, i))
            dve.go(lambda e, i=i: e.bn_aggr(mv[:, which, i, :], stats[:, which, i, :]),
                   done=("fmv", which, i))

    def deviation(which, tiles):
        t = slice(tiles[0], tiles[-1] + 1)
        act.need(("fmv", which, tiles[-1]), "eps2")
        act.go(lambda e: e.activation(dev[:, which, t], mv[:, which, t, 1], ACT.Sqrt,
                                      bias=eps[:, :]), done=("fdev", which, tiles[0]))

    def statistics(which, tiles, ready):
        moments(which, tiles, ready)
        deviation(which, tiles)

    def inverse(which, tiles):
        t = slice(tiles[0], tiles[-1] + 1)
        dve.need(("fdev", which, tiles[0]))
        dve.go(lambda e: e.reciprocal(rstd[:, which, t], dev[:, which, t]),
               done=("frstd", which, tiles[0]))
        dve.need(("frstd", which, tiles[0]))

    def apply_norm(which, i, dst, done):
        dve.go(lambda e: e.tensor_scalar(dst, acc(i), mv[:, which, i, 0:1],
                                         rstd[:, which, i:i + 1], ALU.subtract, ALU.mult),
               done=done)

    def block(tb):
        return range(tb * TT, (tb + 1) * TT)

    def prepare_load(tb):
        for i in block(tb):
            sync.load(lambda e, i=i: e.dma_start(acc(i), attn_dram[i]), ("fa", i),
                      core.dma_sem(f"fa{i % (2 * TT)}"))
            sync.need(("x2", i - 2 * TT) if i >= 2 * TT else None)
            sync.load(lambda e, i=i: e.dma_start(xin(i), x_t[i]), ("fx", i),
                      core.dma_sem(f"fx{i % (2 * TT)}"))

    def prepare(tb):
        first, second = block(tb)[:2], block(tb)[2:]
        pause = (None,) * (2 if tb else 1)
        for tiles in (first, second):
            moments(0, tiles, lambda i: ("fa", i))
            yield
        deviation(0, block(tb))
        yield from pause
        inverse(0, block(tb))
        for tiles in (first, second):
            for i in tiles:
                apply_norm(0, i, acc(i), ("n0", i))
                add_residual(i)
            yield
        yield from pause[1:] * 2
        if 1 <= tb < NTB - 2:
            prepare_load(tb + 2)
        for tiles in (first, second):
            moments(1, tiles, lambda i: ("x2", i))
            yield
        deviation(1, block(tb))
        yield from pause
        inverse(1, block(tb))
        tiles = block(tb)
        for n in range(TT + 1):
            if n < TT:
                i = tiles[n]
                dve.need(("FT", i - 2) if i >= 2 else None)
                apply_norm(1, i, tmp[:, i % 2, :], ("xf", i))
            yield
            if n >= 1:
                transpose_tile(tiles[n - 1])

    def add_residual(i):
        pool.need(("n0", i), ("fx", i), pool.last)
        pool.go(lambda e: e.tensor_tensor(acc(i), acc(i), xin(i), ALU.add),
                done=("x2", i))
        sync.need(("x2", i))
        sync.load(lambda e: e.dma_start(x2_dram[i], acc(i)), ("x2 out", i),
                  core.dma_sem(f"x2o{i % (2 * TT)}"))

    def transpose_tile(i):
        r = i % 2
        pe.need(("xf", i), ("ft low", i - 2) if i >= 2 else None)
        def issue(e, i=i, r=r):
            for k in range(KD):
                ins = e.transpose(t_ps[r][:, k * P:(k + 1) * P],
                                  tmp[:, r, k * P:(k + 1) * P], ident[:, :])
            return ins
        pe.go(issue, done=("FT", i))
        tok = slice(i % TT * P, (i % TT + 1) * P)
        view = t_ps[r][:, :].rearrange("p (k t) -> p k t", k=KD)
        act.need(("FT", i))
        act.go(lambda e, tok=tok, view=view: e.activation(xt_high[i // TT][:, :, tok], view,
                                                          ACT.Copy), done=("ft high", i))
        dve.need(("ft high", i))
        dve.go(lambda e, tok=tok, view=view: e.tensor_tensor(
            xt_low[i // TT][:, :, tok], view, f32(xt_high[i // TT][:, :, tok]), ALU.subtract),
            done=("ft low", i))

    unit = [0]
    unit_of = {}

    def gate_up(g, tb, k):
        h0, hw = hidden(g)
        r, m = g % 2, blocks.index((g, tb)) % 2
        rows = min(P, hw - k * P)
        n = unit[0]
        unit[0] += 1
        b = n % 2
        pe.need(("ft low", (tb + 1) * TT - 1), ("w low", g, 0), ("w low", g, 1),
                ("mid", n - 2) if n >= 2 else None)
        for which, bank in ((0, g_ps[b]), (1, u_ps[b])):
            wh = weight_views(w_high[r][:, which, :], g, which)
            wl = weight_views(w_low[r][:, which, :], g, which)
            cols = slice(k * P, k * P + rows)
            pairs = []
            for d in range(KD):
                pairs += split_passes(wh[:, d, cols], wl[:, d, cols], xt_high[tb][:, d, :],
                                      xt_low[tb][:, d, :])
            pe.go(lambda e, bank=bank, pairs=pairs: mm_chain(e, bank[0:rows, :], pairs),
                  done=("gu", n, which))
        act.need(("gu", n, 0), ("mid", n - 2) if n >= 2 else None)
        act.go(lambda e: e.activation(gate[0:rows, b, :], g_ps[b][0:rows, :], ACT.Silu),
               done=("silu", n))
        dve.need(("silu", n), ("gu", n, 1), ("mid low", n - 2) if n >= 2 else None)
        dve.go(lambda e: e.tensor_tensor(mid[0:rows, b, :], u_ps[b][0:rows, :],
                                         gate[0:rows, b, :], ALU.mult), done=("mid", n))
        at = blocks.index((g, tb))
        act.need(("mid", n), ("D", *blocks[at - 2]) if at >= 2 else None)
        act.go(lambda e: e.activation(mid_high[0:rows, m, k, :], mid[0:rows, b, :],
                                      ACT.Copy), done=("mid high", n))
        pool.need(("mid high", n))
        pool.go(lambda e: e.tensor_tensor(mid_low[0:rows, m, k, :], mid[0:rows, b, :],
                                          f32(mid_high[0:rows, m, k, :]), ALU.subtract),
                done=("mid low", n))
        unit_of[g, tb] = n

    down_turn = [0]
    d_read = [None, None]

    def down(g, tb, t):
        h0, hw = hidden(g)
        r, m = g % 2, blocks.index((g, tb)) % 2
        wh = weight_views(w_high[r][:, 2, :], g, 2)
        wl = weight_views(w_low[r][:, 2, :], g, 2)
        i = tb * TT + t
        b = down_turn[0] % 2
        down_turn[0] += 1
        pe.need(("mid low", unit_of[g, tb]), ("w low", g, 2), d_read[b])
        pairs = []
        for k in range(-(-hw // P)):
            rows = min(P, hw - k * P)
            s = slice(t * P, (t + 1) * P)
            pairs += split_passes(mid_high[0:rows, m, k, s], mid_low[0:rows, m, k, s],
                                  wh[0:rows, k, :], wl[0:rows, k, :])
        name = ("D", g, tb) if t == TT - 1 else ("D", g, tb, t)
        pe.go(lambda e: mm_chain(e, d_ps[b][:, :], pairs), done=name)
        if g == 0:
            act.need(name, ("x2 out", i), ("xf", i))
            act.go(lambda e: e.activation(acc(i), d_ps[b][:, :], ACT.Copy),
                   done=("part", g, i))
        else:
            dve.need(name, ("part", g - 1, i))
            dve.go(lambda e: e.tensor_tensor(acc(i), d_ps[b][:, :], acc(i),
                                             ALU.add), done=("part", g, i))
        d_read[b] = ("part", g, i)

    def finish_load(tb):
        for i in block(tb):
            sync.need(("y", i - 2 * TT) if i >= 2 * TT else ("x2", NT - 2 * TT + i),
                      ("x2 out", i))
            sync.load(lambda e, i=i: e.dma_start(xin(i), x2_dram[i]), ("fx2", i),
                      core.dma_sem(f"fx{i % (2 * TT)}"))

    def finish_block(tb):
        first, second = block(tb)[:2], block(tb)[2:]
        for tiles in (first, second):
            moments(2, tiles, lambda i: ("part", last, i))
            yield
        deviation(2, block(tb))
        yield
        yield
        inverse(2, block(tb))
        for tiles in (first, second):
            finish(tiles, pool)
            yield
        if tb + 2 < NTB:
            finish_load(tb + 2)

    def finish(tiles, adder):
        for i in tiles:
            apply_norm(2, i, acc(i), ("n2", i))
        for i in tiles:
            adder.need(("n2", i), ("fx2", i))
            adder.go(lambda e, i=i: e.tensor_tensor(acc(i), acc(i),
                                                  xin(i), ALU.add),
                   done=("y", i))
            sync.need(("y", i))
            sync.load(lambda e, i=i: e.dma_start(out_t[i], acc(i)), ("out", i),
                      core.dma_sem(f"out{i}"))

    sets = [range(0, 2)] + [range(g, g + 1) for g in range(2, NFG - 2)] + [range(NFG - 2, NFG)]
    blocks = [(g, tb) for groups in sets for tb in range(NTB) for g in groups]
    last = NFG - 1

    prepare_load(0)
    for n, s in enumerate((sg, su, sd)):
        sync.load(lambda e, n=n, s=s: e.dma_start(scale[:, n:n + 1], s.to_broadcast((P, 1))),
                  ("scale", n), core.dma_sem(f"scale{n}"))
    weights_load(0)
    yield
    parts = prepare(0)
    for _ in range(8):
        next(parts)
        yield
    while latents_over not in core.reached:
        yield
    for _ in parts:
        yield
    for n in range(3):
        weights_split(0, n)
        yield
    while attention_over[0] not in core.reached:
        yield
    for lane in (act, dve, pool, sync):
        lane.need(*attention_over, *output_over)

    waiting = []

    def advance(parts=1):
        for _ in range(parts):
            while waiting and next(waiting[0], "over") == "over":
                waiting.pop(0)

    def pace(g, tb):
        return 3 if g >= 2 else 4 if tb else 5

    def complete(work):
        while work in waiting:
            advance()

    def weights(g):
        for n in range(3):
            weights_split(g, n)
            yield
        if g + 1 < NFG:
            weights_load(g + 1)

    weights_load(1)
    prepare_load(1)
    prepare_load(2)
    weights_of = {1: weights(1)}
    tokens_of = {tb: prepare(tb) for tb in range(1, NTB)}
    waiting.append(weights_of[1])
    for n in range(len(blocks) + 1):
        g, tb = blocks[n] if n < len(blocks) else (None, None)
        if g is not None:
            if g == 0:
                if tb + 1 < NTB:
                    waiting.append(tokens_of[tb + 1])
                complete(tokens_of.get(tb))
            complete(weights_of.get(g))
            gate_up(g, tb, 0)
            if n == 0:
                pe.need(*attention_over)
            advance(pace(g, tb))
            if g == last and tb < 2:
                finish_load(tb)
        if n >= 1:
            g0, tb0 = blocks[n - 1]
            for t in range(TT):
                down(g0, tb0, t)
                if g0 == last and tb0 == NTB - 1:
                    i = tb0 * TT + t
                    statistics(2, range(i, i + 1), lambda i: ("part", last, i))
                    if t >= 1:
                        inverse(2, range(i - 1, i))
                        finish(range(i - 1, i), dve)
                else:
                    advance()
            if g0 == last and tb0 < NTB - 1:
                waiting.append(finish_block(tb0))
            if tb0 == NTB - 1 and g0 + 2 < NFG:
                weights_of[g0 + 2] = weights(g0 + 2)
                waiting.append(weights_of[g0 + 2])
                if n + 1 < len(blocks) and blocks[n + 1][0] == g0 + 2:
                    complete(weights_of[g0 + 2])
        if g is not None:
            for k in range(1, -(-hidden(g)[1] // P)):
                gate_up(g, tb, k)
                advance(pace(g, tb))
        if n == len(blocks) - 1:
            while waiting:
                advance()
    inverse(2, range(NT - 1, NT))
    finish(range(NT - 1, NT), dve)
    for i in range(NT):
        sync.need(("out", i), ("x2 out", i), ("attn out", i // JT, i % JT))
    for g in range(NG):
        sync.need(("m out", g))


def _tables():
    import numpy as np
    exponents = np.arange(0, ROPE, 2, dtype=np.float32) / np.float32(ROPE)
    freqs = np.float32(1.0) / np.power(np.float32(10000.0), exponents)
    angles = np.outer(np.arange(SEQ, dtype=np.float32), freqs.astype(np.float32))
    cos, sin = np.cos(angles), np.sin(angles)
    rope_k = np.concatenate([cos, cos, -sin, sin], axis=1).astype(np.float32)
    scale = -1.0 / np.sqrt(np.float64(NOPE + ROPE))
    rope_q = np.zeros((2, P, SEQ), np.float32)
    rope_q[0, 0:KVL] = scale
    rope_q[0, KVL:P] = np.concatenate([cos.T, cos.T]) * scale
    rope_q[1, KVL:P] = np.concatenate([sin.T, -sin.T]) * scale
    far = np.zeros((P, SEQ), np.float32)
    far[:, SEQ - P:] = np.where(np.arange(P)[None, :] > np.arange(P)[:, None], FAR, 0.0)
    return rope_k, rope_q, far


def kernel(**inputs):
    import numpy as np
    import concourse.bacc as bacc
    from concourse.bass_utils import run_bass_kernel_spmd

    get = lambda n: np.asarray(inputs[n])
    evens_odds = lambda a: np.concatenate([a[..., 0::2, :], a[..., 1::2, :]], axis=-2)
    wkv_a = get("L0_attn_wkv_a")
    wq_b = get("L0_attn_wq_b").reshape(NH, NOPE + ROPE, QL)
    wkv_b = get("L0_attn_wkv_b").reshape(NH, NOPE + VD, KVL)
    wa = np.concatenate([get("L0_attn_wq_a"), wkv_a[:KVL], evens_odds(wkv_a[KVL:])], axis=0).T
    twice = lambda a: np.concatenate([a, a[..., P:QL]], axis=-1)
    wqn = twice(wq_b[:, :NOPE]).transpose(1, 0, 2)
    wqp = twice(evens_odds(wq_b[:, NOPE:])).reshape(NH * ROPE, 2, P).transpose(2, 1, 0)
    rope_k, rope_q, far = _tables()
    arrays = {
        "x": get("L0_attn_x").reshape(TOKENS, DM),
        "wa": wa, "wqn": wqn, "wqp": wqp,
        "wk": wkv_b[:, :NOPE].transpose(1, 0, 2),
        "wv": wkv_b[:, NOPE:].transpose(1, 0, 2),
        "wo": get("L0_attn_wo").T.reshape(NH, VD, DM).transpose(1, 0, 2),
        "qw": twice(get("L0_attn_q_norm_w")).reshape(2, P).T,
        "kvw": get("L0_attn_kv_norm_w").reshape(1, KVL),
        "rope_k": rope_k, "rope_q": rope_q, "far": far,
        "wg": get("L0_ffn_w_gate").T, "wu": get("L0_ffn_w_up").T, "wd": get("L0_ffn_w_down").T,
        "sg": get("L0_ffn_scale_gate").reshape(1, 1),
        "su": get("L0_ffn_scale_up").reshape(1, 1),
        "sd": get("L0_ffn_scale_down").reshape(1, 1),
    }
    arrays = {n: np.ascontiguousarray(a) for n, a in arrays.items()}
    nc = bacc.Bacc("TRN2", target_bir_lowering=False, num_devices=1)
    args = [nc.dram_tensor(n, a.shape, mybir.dt.from_np(a.dtype), kind="ExternalInput").ap()
            for n, a in arrays.items()]
    out = nc.dram_tensor("out", (TOKENS, DM), F32, kind="ExternalOutput").ap()
    layer_kernel(nc, *args, out)
    result = run_bass_kernel_spmd(nc, [arrays], core_ids=[0])
    return result.results[0]["out"].reshape(BATCH, SEQ, DM)
```
